# Optimizing a Trainium2 kernel written in Bass

```python
import numpy as np
import jax
import jax.numpy as jnp

def _softmax(x, axis=-1):
    return jax.nn.softmax(x, axis=axis)

def _gelu(x):
    return jax.nn.gelu(x, approximate=True)

def _silu(x):
    return jax.nn.silu(x)

def _sigmoid(x):
    return jax.nn.sigmoid(x)

def _layernorm(x, axis=-1, eps=1e-05):
    m = jnp.mean(x, axis=axis, keepdims=True)
    v = jnp.var(x, axis=axis, keepdims=True)
    return (x - m) / jnp.sqrt(v + eps)

def _scatter_add(tgt, idx, src, axis=0):
    return tgt.at[idx].add(src)

def _segment_sum(src, seg, n):
    return jax.ops.segment_sum(src, seg, n)
kernel_name = 'mk_gnn_preln_d2_gnn_r8_e4f5ab'

def setup_inputs(seed: int=0):
    np.random.seed(seed)
    _w = jnp.asarray

    def _rec_inputs():
        import jax
        import jax.numpy as jnp
        _gk = jax.random.key(seed)
        x = -0.0001006 + 1 * jax.random.normal(jax.random.fold_in(_gk, 1), (6250, 96), jnp.float32)
        _s = jax.random.randint(jax.random.fold_in(_gk, 2), (50000,), 0, 6250, jnp.int32)
        _d = jax.random.randint(jax.random.fold_in(_gk, 3), (50000,), 0, 6250, jnp.int32)
        _loop = jnp.arange(6250, dtype=jnp.int32)
        src = jnp.concatenate([_s, _d, _loop])
        dst = jnp.concatenate([_d, _s, _loop])
        _o = jnp.argsort(dst, stable=True)
        src = src[_o]
        dst = dst[_o]
        return (x, src, dst)
    x, src, dst = _rec_inputs()

    def _L0_gnn_setup():
        import jax, jax.numpy as jnp
        import numpy as np
        N_NODES = 6250
        N_EDGES = 100000
        D_MODEL = 96
        HEADS = 4
        key = jax.random.key(seed)
        ks = jax.random.split(key, 6)
        scale = 1.0 / np.sqrt(D_MODEL)
        return {'embeds': jax.random.normal(ks[0], (N_NODES, D_MODEL), dtype=jnp.float32), 'qW': jax.random.normal(ks[1], (D_MODEL, D_MODEL), dtype=jnp.float32) * scale, 'kW': jax.random.normal(ks[2], (D_MODEL, D_MODEL), dtype=jnp.float32) * scale, 'vW': jax.random.normal(ks[3], (D_MODEL, D_MODEL), dtype=jnp.float32) * scale, 'rows': jax.random.randint(ks[4], (N_EDGES,), 0, N_NODES, dtype=jnp.int32), 'cols': jax.random.randint(ks[5], (N_EDGES,), 0, N_NODES, dtype=jnp.int32)}
    _L0_gnn_all = _L0_gnn_setup()
    _L0_gnn_in = {k: v for k, v in _L0_gnn_all.items() if k in ('qW', 'kW', 'vW')}
    del _L0_gnn_all

    def _L1_gnn_setup():
        import jax, jax.numpy as jnp
        import numpy as np
        N_NODES = 6250

        def mish(y):
            return y * jnp.tanh(jax.nn.softplus(y))

        def gcn_conv(x, edge_index, W, b):
            n = x.shape[0]
            loop = jnp.arange(n, dtype=edge_index.dtype)
            src = jnp.concatenate([edge_index[0], loop])
            dst = jnp.concatenate([edge_index[1], loop])
            h = x @ W
            deg = jax.ops.segment_sum(jnp.ones_like(dst, dtype=h.dtype), dst, num_segments=n)
            dinv = jnp.where(deg > 0, jax.lax.rsqrt(deg), 0.0)
            norm = dinv[src] * dinv[dst]
            msg = h[src] * norm[:, None]
            agg = jax.ops.segment_sum(msg, dst, num_segments=n)
            return agg + b
        key = jax.random.key(seed)
        ks = jax.random.split(key, 5)
        d_in, d_out = (96, 96)
        x = jax.random.normal(ks[0], (N_NODES, d_in), dtype=jnp.float32)
        edge_index = jax.random.randint(ks[1], (2, 100000), 0, N_NODES, dtype=jnp.int64)
        W_gcn = jax.random.normal(ks[2], (d_in, d_out), dtype=jnp.float32) / np.sqrt(d_in)
        b_gcn = jnp.zeros((d_out,), dtype=jnp.float32)
        W_lin = jax.random.normal(ks[3], (d_in, d_out), dtype=jnp.float32) / np.sqrt(d_in)
        b_lin = jnp.zeros((d_out,), dtype=jnp.float32)
        return {'x': x, 'edge_index': edge_index, 'W_gcn': W_gcn, 'b_gcn': b_gcn, 'W_lin': W_lin, 'b_lin': b_lin}
    _L1_gnn_all = _L1_gnn_setup()
    _L1_gnn_in = {k: v for k, v in _L1_gnn_all.items() if k in ('W_gcn', 'b_gcn', 'W_lin', 'b_lin')}
    del _L1_gnn_all
    return {'x': x, 'src': src, 'dst': dst, 'L0_gnn_qW': _L0_gnn_in['qW'], 'L0_gnn_kW': _L0_gnn_in['kW'], 'L0_gnn_vW': _L0_gnn_in['vW'], 'L1_gnn_W_gcn': _L1_gnn_in['W_gcn'], 'L1_gnn_b_gcn': _L1_gnn_in['b_gcn'], 'L1_gnn_W_lin': _L1_gnn_in['W_lin'], 'L1_gnn_b_lin': _L1_gnn_in['b_lin']}

def reference(x, src, dst, L0_gnn_qW, L0_gnn_kW, L0_gnn_vW, L1_gnn_W_gcn, L1_gnn_b_gcn, L1_gnn_W_lin, L1_gnn_b_lin):
    import jax
    import jax.numpy as jnp

    def _L0_gnn_ref(embeds, qW, kW, vW, rows, cols):
        import jax, jax.numpy as jnp
        import numpy as np
        N_NODES = 6250
        N_EDGES = 100000
        D_MODEL = 96
        HEADS = 4
        nvar, d = embeds.shape
        dh = d // HEADS
        e = rows.shape[0]
        q = (embeds[rows] @ qW).reshape(e, HEADS, dh)
        k = (embeds[cols] @ kW).reshape(e, HEADS, dh)
        v = (embeds[cols] @ vW).reshape(e, HEADS, dh)
        scores = jnp.clip(jnp.einsum('ehd,ehd->eh', q, k), -10.0, 10.0)
        exp_s = jnp.exp(scores)
        norms = jax.ops.segment_sum(exp_s, rows, num_segments=nvar)[rows]
        w = exp_s / (norms + 1e-08)
        res = jax.ops.segment_sum(w[:, :, None] * v, rows, num_segments=nvar).reshape(nvar, d)
        return embeds + res

    def _L1_gnn_ref(x, edge_index, W_gcn, b_gcn, W_lin, b_lin):
        import jax, jax.numpy as jnp
        import numpy as np
        N_NODES = 6250

        def mish(y):
            return y * jnp.tanh(jax.nn.softplus(y))

        def gcn_conv(x, edge_index, W, b):
            n = x.shape[0]
            loop = jnp.arange(n, dtype=edge_index.dtype)
            src = jnp.concatenate([edge_index[0], loop])
            dst = jnp.concatenate([edge_index[1], loop])
            h = x @ W
            deg = jax.ops.segment_sum(jnp.ones_like(dst, dtype=h.dtype), dst, num_segments=n)
            dinv = jnp.where(deg > 0, jax.lax.rsqrt(deg), 0.0)
            norm = dinv[src] * dinv[dst]
            msg = h[src] * norm[:, None]
            agg = jax.ops.segment_sum(msg, dst, num_segments=n)
            return agg + b
        x_gcn = gcn_conv(x, edge_index, W_gcn, b_gcn)
        x_skip = x @ W_lin + b_lin
        return mish(x_gcn + x_skip)
    edge_index = jnp.stack([src, dst])
    h = jnp.maximum(_layernorm(x, axis=-1), 0.0)
    x = x + _L0_gnn_ref(h, L0_gnn_qW, L0_gnn_kW, L0_gnn_vW, src, dst)
    h = jnp.maximum(_layernorm(x, axis=-1), 0.0)
    x = x + _L1_gnn_ref(h, edge_index, L1_gnn_W_gcn, L1_gnn_b_gcn, L1_gnn_W_lin, L1_gnn_b_lin)
    return x

_drawn_inputs = setup_inputs


def setup_inputs(seed=0):
    import zlib

    import numpy as np

    out = dict(_drawn_inputs(seed))
    spreads = {'L1_gnn_b_gcn': (0.0, 0.1), 'L1_gnn_b_lin': (0.0, 0.1)}
    factors = {}
    for name, (base, spread) in spreads.items():
        noise = np.random.default_rng([zlib.crc32(name.encode()), seed]).standard_normal(out[name].shape)
        drawn = base * np.exp(spread * noise) if base else spread * noise
        out[name] = jnp.asarray(drawn.astype(out[name].dtype))
    for name, factor in factors.items():
        out[name] = (out[name] * factor).astype(out[name].dtype)
    return out
```

```python
from contextlib import ExitStack

import concourse.bass as bass
from concourse import mybir

ALU = mybir.AluOpType
ACT = mybir.ActivationFunctionType
AX = mybir.AxisListType
F32 = mybir.dt.float32
BF16 = mybir.dt.bfloat16
I32 = mybir.dt.int32
U8 = mybir.dt.uint8

P = 128
HEADS = 4
EPS = 1e-5
CLIP = 10.0
FEED = 16
GRP = 4
GPI = 4
TPI = GRP * GPI
BLOCKS = 2


class Chain:

    def __init__(self, eng, sem):
        self.eng, self.sem, self.n = eng, sem, 0

    def __call__(self, ins):
        ins.then_inc(self.sem, 1)
        self.n += 1

    def wait(self, but=0):
        if self.n > but:
            self.eng.wait_ge(self.sem, self.n - but)

    def link(self, ins):
        self(ins)
        self.wait()


def gnn_kernel(nc, x, src, dst, qW, kW, vW, W_gcn, b_gcn, W_lin, b_lin, out):
    N, D = x.shape
    E = src.shape[0]
    DH = D // HEADS
    MSG = D + HEADS
    NB = -(-N // P)
    NS = NB + 1
    FULL = N // P
    REST = N - FULL * P
    NCOL = -(-E // (P * 2 * FEED)) * 2 * FEED
    LAST = E - (P - 1) * NCOL
    BC = NCOL // BLOCKS
    PAD_KEY = NB * P
    NT = -(-((E + NB * (P - 1)) // P) // TPI) * TPI
    NTP = NT + TPI
    SLOT_TILES = NT + -(-(P * NCOL - E) // P)
    SLOTS = SLOT_TILES * P
    GROUPS = NT // P + 1
    TAIL = NT - (GROUPS - 1) * P
    HT = NTP // 2
    HIGHEST_START = SLOTS - P
    ITERS = NT // TPI
    assert 0 < LAST <= NCOL and BC <= 512 and HT <= 512 and 0 < TAIL < P
    assert E + P * (NT - -(-E // P)) <= SLOTS and P * NCOL <= SLOTS

    ctx = ExitStack()
    with ctx:
        def sb(name, shape, dt=F32):
            return ctx.enter_context(nc.sbuf_tensor(name, shape, dt))

        def ps(name):
            return ctx.enter_context(nc.psum_tensor(name, [P, 512], F32))

        def sem(name):
            return ctx.enter_context(nc.semaphore(name))

        kv_table = nc.dram_tensor("kv_table", [NS * P, 2 * D], F32, kind="Internal").ap()
        g_table = nc.dram_tensor("g_table", [NS * P, D], F32, kind="Internal").ap()
        sorted0 = nc.dram_tensor("sorted0", [SLOTS, 2], I32, kind="Internal").ap()
        list1 = nc.dram_tensor("list1", [SLOTS, 2], I32, kind="Internal").ap()
        sorted1 = nc.dram_tensor("sorted1", [NT * P, 2], I32, kind="Internal").ap()

        X = sb("X", [P, NS, D])
        H = sb("H", [P, NS, D])
        Q = sb("Q", [P, NS, D])
        T1 = sb("T1", [P, NS, D])
        big = sb("big", [P, max(NS * (MSG + D), NS * NCOL // 4)])
        sums = big[:, 0:NS * MSG].rearrange("p (b m) -> p b m", b=NS)
        G = big[:, NS * MSG:NS * (MSG + D)].rearrange("p (b m) -> p b m", b=NS)
        member = big[:, 0:NS * NCOL // 4].bitcast(U8).rearrange("p (b c) -> p b c", b=NS)

        t1f = T1[:, :, :].rearrange("p b d -> p (b d)")
        src_i = t1f[:, 0:NCOL].bitcast(I32)
        dst_i = t1f[:, NCOL:2 * NCOL].bitcast(I32)
        nxt_i = t1f[:, 2 * NCOL:3 * NCOL].bitcast(I32)
        bkt_i = t1f[:, 3 * NCOL:4 * NCOL].bitcast(I32)
        slot_f = t1f[:, 4 * NCOL:5 * NCOL]
        bkt_b = sb("bkt_b", [P, NCOL], BF16)
        low_b = sb("low_b", [P, NCOL], BF16)
        slot0 = sb("slot0", [P, NCOL], I32)
        slot1 = sb("slot1", [P, NCOL], I32)
        pair0 = sb("pair0", [P, NCOL, 2], I32)
        pair1 = sb("pair1", [P, NCOL, 2], I32)
        slot_ring = sb("slot_ring", [P, 2, FEED], I32)
        pair_ring = sb("pair_ring", [P, 2, FEED, 2], I32)

        rows = sb("rows", [P, GROUPS, 2 * P], I32)
        rows_f = sb("rows_f", [P, 2 * P])
        key_l = sb("key_l", [P, NTP])
        partner = sb("partner", [P, NTP], I32)
        base0 = sb("base0", [P, NTP])
        base1 = sb("base1", [P, NTP])
        tile_b0 = sb("tile_b0", [1, NTP], I32)
        tile_b1 = sb("tile_b1", [1, NTP], I32)
        tile_s1 = sb("tile_s1", [1, NTP], I32)
        qf = Q[:, :, :].rearrange("p b d -> p (b d)")
        iota_t = qf[:, 0:NTP]
        begun = qf[:, NTP:2 * NTP]

        iota_n = sb("iota_n", [P, P])
        iota_b = sb("iota_b", [P, P], BF16)
        diff = sb("diff", [P, P])
        ident = sb("ident", [P, P])
        before = sb("before", [P, P])
        ones = sb("ones", [P, P])
        zero_b = sb("zero_b", [P, P], BF16)
        qkv_w = sb("qkv_w", [D, 3 * D])
        gl_w = sb("gl_w", [D, 2 * D])
        bias2 = sb("bias2", [P, 2, D])

        count = sb("count", [P, BLOCKS, NS])
        csum = sb("csum", [P, NS])
        n_all = sb("n_all", [P, NS])
        prior = sb("prior", [P, NS])
        n_tile = sb("n_tile", [P, NS])
        n_tile_i = sb("n_tile_i", [P, NS], I32)
        tile_end = sb("tile_end", [P, NS])
        edge_end = sb("edge_end", [P, NS])
        excess = sb("excess", [P, NS])
        first = sb("first", [P, BLOCKS, NS])
        cols = sb("cols", [NS, 2])
        flag = sb("flag", [P, 2])
        flag_i = sb("flag_i", [1, 1], I32)
        mean = sb("mean", [P, NS])
        var = sb("var", [P, NS])
        rstd = sb("rstd", [P, NS])
        deg = sb("deg", [P, NS])
        root = sb("root", [P, NS])
        dinv = sb("dinv", [P, NS])

        stage = sb("stage", [P, 2, D])
        hT = sb("hT", [D, 2, P])
        kv_stage = sb("kv_stage", [P, 2, 2 * D])
        got = sb("got", [P, TPI, 2 * D])
        gotf = got[:, :, :].rearrange("p t w -> p (t w)")
        n_low, n_bkt = FEED * P, FEED * NS
        low_hot = gotf[:, 0:n_low].bitcast(BF16).rearrange("p (h c n) -> p h c n", h=2, n=P)
        bkt_hot = gotf[:, n_low:n_low + n_bkt].bitcast(BF16).rearrange("p (h c n) -> p h c n", h=2, n=NS)
        idx_ring = sb("idx_ring", [P, TPI], I32)
        p0f = pair0[:, :, :].rearrange("p c k -> p (c k)").bitcast(F32)
        p1f = pair1[:, :, :].rearrange("p c k -> p (c k)").bitcast(F32)
        n_hot = GRP * P
        hot = p0f[:, 0:2 * n_hot].rearrange("p (k t n) -> p k t n", k=2, n=P)
        prod = p0f[:, 2 * n_hot:2 * n_hot + GRP * D].rearrange("p (t d) -> p t d", d=D)
        hotT = p1f[:, 0:2 * n_hot].rearrange("p (k n) -> p k n", k=2)
        score = sb("score", [P, 2, GRP * HEADS])
        msg = sb("msg", [P, 2, GRP, MSG])

        psA = [ps("psA0"), ps("psA1")]
        psB = [ps("psB0"), ps("psB1")]
        psC = [ps("psC0"), ps("psC1")]
        psD = ps("psD")
        psE = ps("psE")

        s_edges = sem("edges_loaded")
        s_x = sem("x_loaded")
        s_w = sem("weights_loaded")
        s_pads = sem("pads_set")
        s_iota = sem("iota_made")
        s_fill = sem("lists_filled")
        s_const = sem("constants_made")
        s_count = sem("counts_made")
        s_meta = sem("offsets_on_pe")
        s_cols = sem("rows_for_columns")
        s_colT = sem("columns_turned")
        s_begun = sem("begun_made")
        s_tile = sem("tile_data_on_pe")
        s_tiled = sem("tile_data_kept")
        s_slot = sem("slots_made")
        s_pair = sem("pairs_made")
        s_v = sem("vector_chain")
        s_vf = sem("vector_chain_unsorted")
        s_flagp = sem("disorder_counted")
        s_flag = sem("flag_made")
        s_fed = [sem("fed_a"), sem("fed_b")]
        s_scat = [sem("scattered_a"), sem("scattered_b")]
        s_fedf = [sem("fed1_a"), sem("fed1_b")]
        s_scatf = [sem("scattered1_a"), sem("scattered1_b")]
        s_slotf = sem("slots1_made")
        s_list1 = sem("list1_written")
        s_var = [sem("variance0"), sem("variance1")]
        s_root = [sem("root0"), sem("root1")]
        s_degr = sem("degree_plus_one")
        s_degroot = sem("degree_root")
        s_pstage = [sem("p_staged0"), sem("p_staged1")]
        s_pT = [sem("p_turned0"), sem("p_turned1")]
        s_phT = [sem("p_kept0"), sem("p_kept1")]
        s_pmm = [sem("p_product0"), sem("p_product1")]
        s_pq = [sem("p_first_out0"), sem("p_first_out1")]
        s_pkv = [sem("p_second_out0"), sem("p_second_out1")]
        s_tab = [[sem("table0_a"), sem("table0_b")], [sem("table1_a"), sem("table1_b")]]
        s_hots = sem("degree_hots")
        s_degmm = sem("degree_products")
        s_rows = [sem("rows0_loaded"), sem("rows1_loaded")]
        s_rowf = [sem("rows0_float"), sem("rows1_float")]
        s_rowT = [sem("rows0_turned"), sem("rows1_turned")]
        s_rowk = [sem("rows0_kept"), sem("rows1_kept")]
        s_align = sem("tile_rows_written")
        s_zero = sem("degree_zeroed")
        s_add = [sem("tiles_added0"), sem("tiles_added1")]
        s_idx = [sem("indices0"), sem("indices1")]
        s_got = [[sem(f"gathered{k}_{g}") for g in range(GPI)] for k in range(2)]
        s_hot = [sem("hot0"), sem("hot1")]
        s_hotp = sem("hot_turned")
        s_hotT = sem("hot_turned_kept")
        s_q = sem("queries_of_edges")
        s_prod = sem("query_key_products")
        s_red = sem("scores_summed")
        s_score = sem("scores_clipped")
        s_exp = sem("exponentials")
        s_msg = sem("messages_made")
        s_part = [sem("bucket_parts0"), sem("bucket_parts1")]
        s_y = sem("final_exp_in")
        s_ye = sem("final_exp_out")
        s_fin = sem("result_made")
        s_out = sem("result_stored")
        s_pool = sem("pool_waited")

        def per_p(flat, n=NCOL):
            return flat.rearrange("(p c) -> p c", c=n)

        block = ctx.enter_context(nc.Block())

        @block.sync
        def _(sp):
            sp.wait_ge(s_pads, 1)
            body = (P - 1) * NCOL
            sp.dma_start(src_i[0:P - 1, :], per_p(src[0:body])).then_inc(s_edges, 16)
            sp.dma_start(src_i[P - 1:P, 0:LAST], src[body:E].rearrange("(p c) -> p c", p=1)).then_inc(s_edges, 16)
            sp.dma_start(dst_i[0:P - 1, :], per_p(dst[0:body])).then_inc(s_edges, 16)
            sp.dma_start(dst_i[P - 1:P, 0:LAST], dst[body:E].rearrange("(p c) -> p c", p=1)).then_inc(s_edges, 16)
            sp.dma_start(nxt_i[0:P - 1, :], per_p(dst[1:body + 1])).then_inc(s_edges, 16)
            sp.dma_start(nxt_i[P - 1:P, 0:LAST - 1], dst[body + 1:E].rearrange("(p c) -> p c", p=1)).then_inc(s_edges, 16)
            flat_rows = rows[:, :, :].rearrange("p g c -> p (g c)")
            for dram in (sorted0, list1):
                sp.dma_start(dram.rearrange("(p s) c -> p (s c)", p=P),
                             flat_rows[:, 0:2 * SLOT_TILES]).then_inc(s_fill, 16)

            def feed(slots, pairs, fed, scattered, made):
                def one(i, first):
                    for h in range(2):
                        if not first:
                            sp.wait_ge(scattered[h], i * (16 * FEED))
                        c = i * (2 * FEED) + h * FEED
                        sp.dma_start(slot_ring[:, h, :], slots[:, bass.ds(c, FEED)]).then_inc(fed[h], 16)
                        sp.dma_start(pair_ring[:, h, :, :].rearrange("p c k -> p (c k)"),
                                     pairs[:, bass.ds(c, FEED), :].rearrange("p c k -> p (c k)")).then_inc(fed[h], 16)
                per = BC // (2 * FEED)
                for b in range(BLOCKS):
                    sp.wait_ge(made, b + 1)
                    if b == 0:
                        one(0, True)
                    with sp.Fori(b * per + (b == 0), (b + 1) * per) as i:
                        one(i, False)

            sp.wait_ge(s_pair, 1)
            feed(slot0, pair0, s_fed, s_scat, s_slot)

            sp.wait_ge(s_flag, 1)
            sp.wait_ge(s_pair, 2)
            sp.wait_ge(s_fill, 32)
            unsorted = sp.value_load(flag_i[0:1, 0:1], min_val=0, max_val=1)
            with sp.If(unsorted > 0):
                feed(slot1, pair1, s_fedf, s_scatf, s_slotf)
                for h in range(2):
                    sp.wait_ge(s_scatf[h], 16 * NCOL // 2)
            with sp.Else():
                sp.dma_start(list1[0:P * NCOL, :].rearrange("(p c) k -> p (c k)", p=P),
                             pair1[:, :, :].rearrange("p c k -> p (c k)")).then_inc(s_list1, 16)
                sp.wait_ge(s_list1, 16)

            def load_rows(listed, k):
                head = (GROUPS - 1) * P
                sp.dma_start(rows[:, 0:GROUPS - 1, :],
                             listed[0:head * P, :].rearrange("(g t l) c -> t g (l c)", t=P, l=P)).then_inc(s_rows[k], 16)
                sp.dma_start(rows[0:TAIL, GROUPS - 1, :],
                             listed[head * P:NT * P, :].rearrange("(t l) c -> t (l c)", l=P)).then_inc(s_rows[k], 16)

            for h in range(2):
                sp.wait_ge(s_scat[h], 16 * NCOL // 2)
            load_rows(sorted0, 0)

            sp.wait_ge(s_tiled, 2)
            sorted1_rows = sorted1.rearrange("(t l) c -> t (l c)", l=P)
            list1_flat = list1.rearrange("s c -> (s c)").rearrange("(a f) -> a f", a=1)
            with sp.Fori(0, NT) as t:
                start = sp.value_load(tile_s1[0:1, bass.ds(t, 1)], min_val=0, max_val=HIGHEST_START)
                sp.dma_start(sorted1_rows[bass.ds(t, 1), :],
                             list1_flat[:, bass.ds(start * 2, 2 * P)]).then_inc(s_align, 16)
            sp.wait_ge(s_align, 16 * NT)
            sp.wait_ge(s_rowf[0], GROUPS)
            load_rows(sorted1, 1)

            sp.wait_ge(s_fin, 1)
            sp.dma_start(out[0:FULL * P, :].rearrange("(b p) d -> p b d", p=P), T1[:, 0:FULL, :]).then_inc(s_out, 16)
            sp.dma_start(out[FULL * P:N, :], T1[0:REST, FULL, :]).then_inc(s_out, 16)
            sp.wait_ge(s_out, 32)

        @block.gpsimd
        def _(pool):
            nc.gpsimd.iota(iota_t, [[1, NTP]], base=0, channel_multiplier=0,
                           allow_small_or_imprecise_dtypes=True).then_inc(s_iota, 1)
            nc.gpsimd.iota(iota_n[:], [[1, P]], base=0, channel_multiplier=0,
                           allow_small_or_imprecise_dtypes=True).then_inc(s_iota, 1)
            nc.gpsimd.iota(diff[:], [[1, P]], base=0, channel_multiplier=-1,
                           allow_small_or_imprecise_dtypes=True).then_inc(s_iota, 1)

            def scatter(target, fed, scattered):
                with pool.Fori(0, NCOL // (2 * FEED)) as i:
                    for h in range(2):
                        pool.wait_ge(fed[h], i * 32 + 32)
                        pool.sem_inc(s_pool, 1)
                        for c in range(FEED):
                            nc.gpsimd.indirect_dma_start(
                                out=target, out_offset=bass.IndirectOffsetOnAxis(ap=slot_ring[:, h, c:c + 1], axis=0),
                                in_=pair_ring[:, h, c, :], in_offset=None).then_inc(scattered[h], 16)

            pool.wait_ge(s_fill, 32)
            scatter(sorted0, s_fed, s_scat)
            pool.wait_ge(s_flag, 1)
            unsorted = pool.value_load(flag_i[0:1, 0:1], min_val=0, max_val=1)
            with pool.If(unsorted > 0):
                scatter(list1, s_fedf, s_scatf)
            with pool.Else():
                pool.wait_ge(s_fill, 32)

            def gathers(k, table, width, free):
                def one(i, first):
                    for g in range(GPI):
                        if g % 2 == 0:
                            pool.wait_ge(s_idx[k], i * 2 + (g // 2 + 1))
                        if not first:
                            pool.wait_ge(free, i * GPI + (g + 1 - GPI))
                        pool.sem_inc(s_pool, 1)
                        for j in range(GRP):
                            n = g * GRP + j
                            nc.gpsimd.indirect_dma_start(
                                out=got[:, n, 0:width], out_offset=None, in_=table,
                                in_offset=bass.IndirectOffsetOnAxis(ap=idx_ring[:, n:n + 1], axis=0)).then_inc(s_got[k][g], 16)
                one(0, True)
                with pool.Fori(1, ITERS) as i:
                    one(i, False)

            for h in range(2):
                pool.wait_ge(s_tab[0][h], 16 * (NS // 2))
            gathers(0, kv_table, 2 * D, s_msg)
            for h in range(2):
                pool.wait_ge(s_tab[1][h], 16 * (NS // 2))
            gathers(1, g_table, D, s_part[1])

        @block.scalar
        def _(act):
            act.wait_ge(s_pads, 1)
            act.dma_start(X[:, 0:FULL, :], x[0:FULL * P, :].rearrange("(b p) d -> p b d", p=P)).then_inc(s_x, 16)
            act.dma_start(X[0:REST, FULL, :], x[FULL * P:N, :]).then_inc(s_x, 16)
            for n, w in enumerate((qW, kW, vW)):
                act.dma_start(qkv_w[:, n * D:(n + 1) * D], w).then_inc(s_w, 16)
            for n, w in enumerate((W_gcn, W_lin)):
                act.dma_start(gl_w[:, n * D:(n + 1) * D], w).then_inc(s_w, 16)
            for n, b in enumerate((b_gcn, b_lin)):
                act.dma_start(bias2[:, n, :], b.rearrange("(a d) -> a d", a=1).to_broadcast([P, D])).then_inc(s_w, 16)

            def root_of(k):
                act.wait_ge(s_var[k], 1)
                nc.scalar.activation(rstd[:], var[:], ACT.Sqrt).then_inc(s_root[k], 1)

            def project(k, table):
                def one(i, first):
                    for h in range(2):
                        act.wait_ge(s_pT[k], i * 2 + (h + 1))
                        if not first:
                            act.wait_ge(s_pmm[k], i * 2 + (h - 1))
                        nc.scalar.copy(hT[:, h, :], psA[h][0:D, 0:P]).then_inc(s_phT[k], 1)
                        b = i * 2 + h
                        act.wait_ge(s_pkv[k], i * 2 + (h + 1))
                        if k == 0:
                            nc.scalar.copy(Q[:, bass.ds(b, 1), :].rearrange("p a d -> p (a d)"),
                                           psB[h][:, 0:D]).then_inc(s_pq[k], 1)
                        else:
                            nc.scalar.copy(Q[:, bass.ds(b, 1), :].rearrange("p a d -> p (a d)"),
                                           psB[h][:, D:2 * D]).then_inc(s_pq[k], 1)
                        w = 2 * D if k == 0 else D
                        act.dma_start(table.rearrange("(b p) w -> b p w", p=P)[bass.ds(b, 1), :, :].rearrange("a p w -> (a p) w"),
                                      kv_stage[:, h, 0:w]).then_inc(s_tab[k][h], 16)
                one(0, True)
                with act.Fori(1, NS // 2) as i:
                    one(i, False)

            def feed_half(k, i, h):
                nc.scalar.copy(idx_ring[:, h * 8:h * 8 + 8], partner[:, bass.ds(i * TPI + h * 8, 8)]).then_inc(s_idx[k], 1)

            root_of(0)
            project(0, kv_table)
            act.wait_ge(s_degr, 1)
            nc.scalar.activation(root[:], deg[:], ACT.Sqrt).then_inc(s_degroot, 1)

            act.wait_ge(s_rowk[0], GROUPS)
            feed_half(0, 0, 0)
            feed_half(0, 0, 1)

            def attention(i, first):
                for g in range(GPI):
                    p = g % 2
                    G0 = i * GPI + g
                    act.wait_ge(s_hotp, G0 + 2)
                    if not (first and g == 0):
                        act.wait_ge(s_q, G0)
                    nc.scalar.copy(hotT[:, 1 - p, :], psA[1 - p][:, :]).then_inc(s_hotT, 1)
                    act.wait_ge(s_score, G0 + 1)
                    if not (first and g < 2):
                        act.wait_ge(s_part[0], G0 - 1)
                    nc.scalar.activation(msg[:, p, :, D:MSG],
                                         score[:, p, :].rearrange("p (t h) -> p t h", h=HEADS),
                                         ACT.Exp).then_inc(s_exp, 1)
                    if p == 1:
                        act.wait_ge(s_got[0][g - 1], i * 64 + 64)
                        act.wait_ge(s_got[0][g], i * 64 + 64)
                        feed_half(0, i + 1, g // 2)

            act.wait_ge(s_hotp, 1)
            nc.scalar.copy(hotT[:, 0, :], psA[0][:, :]).then_inc(s_hotT, 1)
            attention(0, True)
            with act.Fori(1, ITERS) as i:
                attention(i, False)

            root_of(1)
            project(1, g_table)

            act.wait_ge(s_rowk[1], GROUPS)
            feed_half(1, 0, 0)
            feed_half(1, 0, 1)
            with act.Fori(0, ITERS) as i:
                for h in range(2):
                    act.wait_ge(s_got[1][2 * h], i * 64 + 64)
                    act.wait_ge(s_got[1][2 * h + 1], i * 64 + 64)
                    feed_half(1, i + 1, h)

            act.wait_ge(s_y, 1)
            nc.scalar.activation(H[:, :, :], G, ACT.Exp).then_inc(s_ye, 1)

        @block.tensor
        def _(pe):
            pe.wait_ge(s_const, 1)

            def meta(k):
                pe.wait_ge(s_count, k + 1)
                nc.tensor.matmul(psE[:, 0:NS], before[:], csum[:], start=True, stop=True)
                nc.tensor.matmul(psE[:, 64:64 + NS], ones[:], csum[:], start=True, stop=True).then_inc(s_meta, 1)

            def tiles(k):
                pe.wait_ge(s_cols, k + 1)
                nc.tensor.transpose(psE[0:NS, 128:256], tile_end[:], ident[:])
                nc.tensor.transpose(psE[0:NS, 256:384], excess[:], ident[:]).then_inc(s_colT, 1)
                pe.wait_ge(s_begun, k + 1)
                for m in range(2):
                    nc.tensor.matmul(psC[m][:, 0:HT], ones[0:NB, :], begun[0:NB, m * HT:(m + 1) * HT],
                                     start=True, stop=True)
                    mm = nc.tensor.matmul((psE if m else psD)[0:1, 0:HT], cols[0:NB, 1:2],
                                          begun[0:NB, m * HT:(m + 1) * HT], start=True, stop=True)
                mm.then_inc(s_tile, 1)

            meta(0)
            tiles(0)
            meta(1)
            nc.tensor.matmul(psD[:, 0:1], ones[:], flag[:, 0:1], start=True, stop=True).then_inc(s_flagp, 1)
            tiles(1)

            def project(k, weights, width):
                def one(i, first):
                    for h in range(2):
                        pe.wait_ge(s_pstage[k], i * 2 + (h + 1))
                        if not first:
                            pe.wait_ge(s_phT[k], i * 2 + (h - 1))
                        nc.tensor.transpose(psA[h][0:D, 0:P], stage[:, h, :], ident[:]).then_inc(s_pT[k], 1)
                        pe.wait_ge(s_phT[k], i * 2 + (h + 1))
                        if not first:
                            pe.wait_ge(s_pq[k], i * 2 + (h - 1))
                            pe.wait_ge(s_pkv[k], i * 2 + (h - 1))
                        nc.tensor.matmul(psB[h][:, 0:width], hT[:, h, :], weights[:, 0:width],
                                         start=True, stop=True).then_inc(s_pmm[k], 1)
                one(0, True)
                with pe.Fori(1, NS // 2) as i:
                    one(i, False)

            pe.wait_ge(s_w, 16 * 7)
            project(0, qkv_w, 3 * D)

            pe.wait_ge(s_zero, 1)
            nc.tensor.matmul(psD[:, 0:NS], zero_b[:], zero_b[:, 0:NS], start=True, stop=False, skip_group_check=True)
            with pe.Fori(0, NCOL // (2 * FEED)) as i:
                for h in range(2):
                    pe.wait_ge(s_hots, i * 2 + (h + 1))
                    for c in range(FEED):
                        mm = nc.tensor.matmul(psD[:, 0:NS], low_hot[:, h, c, :], bkt_hot[:, h, c, :],
                                              start=False, stop=False, skip_group_check=True)
                    mm.then_inc(s_degmm, 1)

            def turn_rows(k):
                for g in range(GROUPS):
                    T = P if g < GROUPS - 1 else TAIL
                    pe.wait_ge(s_rowf[k], g + 1)
                    if g >= 2:
                        pe.wait_ge(s_rowk[k], g - 1)
                    nc.tensor.transpose(psA[g % 2][:, 0:T], rows_f[0:T, 0:2 * P:2], ident[0:T, 0:T])
                    nc.tensor.transpose(psA[g % 2][:, P:P + T], rows_f[0:T, 1:2 * P:2],
                                        ident[0:T, 0:T]).then_inc(s_rowT[k], 1)

            turn_rows(0)

            def turn_hot(p, G0):
                pe.wait_ge(s_hot[0], G0 + 1)
                for j in range(GRP):
                    mm = nc.tensor.transpose(psA[p][:, j * P:(j + 1) * P], hot[:, p, j, :], ident[:])
                mm.then_inc(s_hotp, 1)

            def queries(p, i, off, G0):
                pe.wait_ge(s_hotT, G0 + 1)
                for j in range(GRP):
                    b = pe.value_load(tile_b0[0:1, bass.ds(i * TPI + (off * GRP + j), 1)], min_val=0, max_val=NB)
                    mm = nc.tensor.matmul(psB[p][:, j * D:(j + 1) * D], hotT[:, p, j * P:(j + 1) * P],
                                          Q[:, bass.ds(b, 1), :].rearrange("p a d -> p (a d)"), start=True, stop=True)
                mm.then_inc(s_q, 1)

            def attention(i, first):
                for g in range(GPI):
                    p = g % 2
                    G0 = i * GPI + g
                    if not (first and g == 0):
                        pe.wait_ge(s_hotT, G0)
                    turn_hot(1 - p, G0 + 1)
                    if not (first and g == 0):
                        pe.wait_ge(s_prod, G0)
                    queries(1 - p, i, g + 1, G0 + 1)
                    pe.wait_ge(s_msg, G0 + 1)
                    if not (first and g < 2):
                        pe.wait_ge(s_add[0], G0 * GRP + (1 - GRP))
                    for j in range(GRP):
                        mm = nc.tensor.matmul(psC[p][:, j * MSG:(j + 1) * MSG], hot[:, p, j, :], msg[:, p, j, :],
                                              start=True, stop=True)
                    mm.then_inc(s_part[0], 1)

            turn_hot(0, 0)
            queries(0, 0, 0, 0)
            attention(0, True)
            with pe.Fori(1, ITERS) as i:
                attention(i, False)

            project(1, gl_w, 2 * D)
            turn_rows(1)

            def convolve(i, first):
                for g in range(GPI):
                    p = g % 2
                    G0 = i * GPI + g
                    pe.wait_ge(s_hot[1], G0 + 1)
                    pe.wait_ge(s_got[1][g], i * 64 + 64)
                    if not (first and g < 2):
                        pe.wait_ge(s_add[1], G0 * GRP + (1 - GRP))
                    for j in range(GRP):
                        mm = nc.tensor.matmul(psC[p][:, j * D:(j + 1) * D], hot[:, p, j, :],
                                              got[:, g * GRP + j, 0:D], start=True, stop=True)
                    mm.then_inc(s_part[1], 1)

            convolve(0, True)
            with pe.Fori(1, ITERS) as i:
                convolve(i, False)

        @block.vector
        def _(dve):
            v = Chain(dve, s_v)

            nc.vector.memset(t1f[:, 0:3 * NCOL].bitcast(I32), PAD_KEY)
            nc.vector.memset(X[:, FULL:NS, :], 0.0)
            all_rows = rows[:, :, :].rearrange("p g (l c) -> p (g l) c", c=2)
            nc.vector.memset(all_rows[:, :, 0], PAD_KEY)
            nc.vector.memset(all_rows[:, :, 1], 0)
            v.link(nc.vector.memset(ones[:], 1.0))
            v.link(nc.vector.memset(slot_f, 0.0))
            nc.vector.memset(zero_b[:], 0.0).then_inc(s_pads, 1)
            dve.wait_ge(s_iota, 3)
            nc.vector.tensor_scalar(ident[:], diff[:], 0.0, None, ALU.is_equal)
            nc.vector.tensor_copy(iota_b[:], iota_n[:])
            nc.vector.tensor_scalar(before[:], diff[:], 0.0, None, ALU.is_gt).then_inc(s_const, 1)

            def count_edges(c):
                for b in range(BLOCKS):
                    for h in range(NS):
                        ins = nc.vector.tensor_scalar(member[:, h, b * BC:(b + 1) * BC], bkt_b[:, b * BC:(b + 1) * BC],
                                                      float(h), None, ALU.is_equal, ALU.add,
                                                      accum_out=count[:, b, h:h + 1])
                c.link(ins)
                c.link(nc.vector.tensor_tensor(csum[:], count[:, 0, :], count[:, 1, :], ALU.add))

            def bucket_of(c, key):
                c.link(nc.vector.tensor_scalar(bkt_i, key, 7, None, ALU.arith_shift_right))
                c.link(nc.vector.tensor_copy(bkt_b[:], bkt_i))

            def offsets(k):
                dve.wait_ge(s_meta, k + 1)
                v.link(nc.vector.tensor_copy(prior[:], psE[:, 0:NS]))
                v.link(nc.vector.tensor_copy(n_all[:], psE[:, 64:64 + NS]))
                v.link(nc.vector.tensor_scalar(n_tile_i[:], n_all[:], float(P - 1), None, ALU.add))
                v.link(nc.vector.tensor_scalar(n_tile_i[:], n_tile_i[:], 7, None, ALU.arith_shift_right))
                v.link(nc.vector.tensor_copy(n_tile[:], n_tile_i[:]))
                v.link(nc.vector.tensor_tensor_scan(tile_end[:], ones[:, 0:NS], n_tile[:], 0.0, ALU.mult, ALU.add))
                v.link(nc.vector.tensor_tensor_scan(edge_end[:], ones[:, 0:NS], n_all[:], 0.0, ALU.mult, ALU.add))
                nc.vector.scalar_tensor_tensor(out=excess[:], in0=n_tile[:], scalar=-float(P), in1=n_all[:],
                                               op0=ALU.mult, op1=ALU.add).then_inc(s_cols, 1)

            def firsts(c, k):
                if k == 0:
                    c.link(nc.vector.tensor_tensor(first[:, 0, :], tile_end[:], n_tile[:], ALU.subtract))
                    c.link(nc.vector.tensor_scalar(first[:, 0, :], first[:, 0, :], float(P), -1.0, ALU.mult, ALU.add))
                    c.link(nc.vector.memset(first[:, 0, NB:NS], float(NT * P - 1)))
                else:
                    c.link(nc.vector.tensor_tensor(first[:, 0, :], edge_end[:], n_all[:], ALU.subtract))
                    c.link(nc.vector.tensor_scalar(first[:, 0, :], first[:, 0, :], 1.0, -1.0, ALU.mult, ALU.add))
                c.link(nc.vector.tensor_tensor(first[:, 0, :], first[:, 0, :], prior[:], ALU.add))
                c.link(nc.vector.tensor_tensor(first[:, 1, :], first[:, 0, :], count[:, 0, :], ALU.add))

            banks = psA + psB

            def slots(c, out_slots, made):
                for b in range(BLOCKS):
                    cut = slice(b * BC, (b + 1) * BC)
                    for h in range(NS + 1):
                        c.wait(1)
                        if h < NS:
                            c(nc.vector.tensor_tensor_scan(banks[h % 4][:, 0:BC], member[:, h, cut], member[:, h, cut],
                                                                first[:, b, h:h + 1], ALU.add, ALU.bypass))
                        if h > 0:
                            c.wait(1 if h < NS else 0)
                            c(nc.vector.copy_predicated(slot_f[:, cut], member[:, h - 1, cut],
                                                        banks[(h - 1) % 4][:, 0:BC]))
                    c.wait()
                    nc.vector.tensor_copy(out_slots[:, cut], slot_f[:, cut]).then_inc(made, 1)
                dve.wait_ge(made, BLOCKS)

            dve.wait_ge(s_edges, 16 * 6)
            bucket_of(v, src_i)
            count_edges(v)
            nc.vector.tensor_copy(pair0[:, :, 0], src_i).then_inc(s_count, 1)
            nc.vector.tensor_copy(pair0[:, :, 1], dst_i).then_inc(s_pair, 1)
            offsets(0)
            firsts(v, 0)
            slots(v, slot0, s_slot)

            def tile_data(k):
                dve.wait_ge(s_colT, k + 1)
                v.link(nc.vector.tensor_copy(cols[:, 0:1], psE[0:NS, 128:129]))
                v.link(nc.vector.tensor_copy(cols[:, 1:2], psE[0:NS, 256:257]))
                nc.vector.tensor_scalar(begun[0:NS, :], iota_t[0:NS, :], cols[:, 0:1], None, ALU.is_ge).then_inc(s_begun, 1)
                dve.wait_ge(s_tile, k + 1)
                for m in range(2):
                    half = slice(m * HT, (m + 1) * HT)
                    nc.vector.tensor_scalar((base1 if k else base0)[:, half], psC[m][:, 0:HT], float(P), None, ALU.mult)
                    ins = nc.vector.tensor_copy((tile_b1 if k else tile_b0)[:, half], psC[m][0:1, 0:HT])
                    if k == 1:
                        ins = nc.vector.scalar_tensor_tensor(
                            out=tile_s1[:, half], in0=iota_t[0:1, half], scalar=float(P),
                            in1=(psE if m else psD)[0:1, 0:HT], op0=ALU.mult, op1=ALU.add)
                v.link(ins)

            tile_data(0)
            nc.vector.memset(key_l[:, NT:NTP], float(2 * P)).then_inc(s_tiled, 1)

            bucket_of(v, dst_i)
            v.link(nc.vector.tensor_scalar(nxt_i, nxt_i, 7, None, ALU.arith_shift_right))
            v.link(nc.vector.tensor_tensor(slot_f, bkt_i, nxt_i, ALU.is_gt))
            v.link(nc.vector.tensor_reduce(flag[:, 0:1], slot_f, AX.X, ALU.add))
            v.link(nc.vector.tensor_scalar(nxt_i, dst_i, P - 1, None, ALU.bitwise_and))
            v.link(nc.vector.tensor_copy(low_b[:], nxt_i))
            count_edges(v)
            nc.vector.tensor_copy(pair1[:, :, 0], dst_i).then_inc(s_count, 1)
            nc.vector.tensor_copy(pair1[:, :, 1], src_i).then_inc(s_pair, 1)
            dve.wait_ge(s_flagp, 1)
            nc.vector.tensor_scalar(flag_i[:], psD[0:1, 0:1], 1.0, None, ALU.min).then_inc(s_flag, 1)
            offsets(1)
            tile_data(1)
            nc.vector.memset(partner[:, NT:NTP], 0).then_inc(s_tiled, 1)
            dve.wait_ge(s_flag, 1)
            unsorted = dve.value_load(flag_i[0:1, 0:1], min_val=0, max_val=1)
            with dve.If(unsorted > 0):
                f = Chain(dve, s_vf)
                firsts(f, 1)
                slots(f, slot1, s_slotf)
                dve.wait_ge(s_slotf, BLOCKS)
            with dve.Else():
                dve.wait_ge(s_flag, 1)

            Hf, Xf = H[:, :, :], X[:, :, :]

            def wide(t):
                return t[:].rearrange("p (b a) -> p b a", a=1).to_broadcast([P, NS, D])

            def layer_norm(k):
                v.link(nc.vector.tensor_reduce(mean[:], Xf, AX.X, ALU.add))
                v.link(nc.vector.tensor_scalar(mean[:], mean[:], 1.0 / D, None, ALU.mult))
                v.link(nc.vector.tensor_tensor(Hf, Xf, wide(mean), ALU.subtract))
                v.link(nc.vector.tensor_tensor(T1[:, :, :], Hf, Hf, ALU.mult))
                v.link(nc.vector.tensor_reduce(var[:], T1[:, :, :], AX.X, ALU.add))
                nc.vector.tensor_scalar(var[:], var[:], 1.0 / D, EPS, ALU.mult, ALU.add).then_inc(s_var[k], 1)
                dve.wait_ge(s_root[k], 1)
                v.link(nc.vector.reciprocal(rstd[:], rstd[:]))
                v.link(nc.vector.tensor_tensor(Hf, Hf, wide(rstd), ALU.mult))
                v.link(nc.vector.tensor_scalar(Hf, Hf, 0.0, None, ALU.max))

            def project(k):
                def staged(i, h):
                    nc.vector.tensor_copy(stage[:, h, :], H[:, bass.ds(i * 2 + h, 1), :].rearrange("p a d -> p (a d)")
                                          ).then_inc(s_pstage[k], 1)

                def one(i, first):
                    for h in range(2):
                        b = i * 2 + h
                        if not first:
                            dve.wait_ge(s_pT[k], i * 2 + (h - 1))
                        staged(i, h)
                    for h in range(2):
                        b = i * 2 + h
                        dve.wait_ge(s_pmm[k], i * 2 + (h + 1))
                        if not first:
                            dve.wait_ge(s_tab[k][h], i * 16)
                        if k == 0:
                            nc.vector.tensor_copy(kv_stage[:, h, :], psB[h][:, D:3 * D]).then_inc(s_pkv[k], 1)
                        else:
                            nc.vector.tensor_scalar(G[:, bass.ds(b, 1), :].rearrange("p a d -> p (a d)"), psB[h][:, 0:D],
                                                    dinv[:, bass.ds(b, 1)], None, ALU.mult)
                            nc.vector.tensor_scalar(kv_stage[:, h, 0:D], psB[h][:, 0:D],
                                                    dinv[:, bass.ds(b, 1)], None, ALU.mult).then_inc(s_pkv[k], 1)
                one(0, True)
                with dve.Fori(1, NS // 2) as i:
                    one(i, False)

            dve.wait_ge(s_x, 32)
            layer_norm(0)
            project(0)

            nc.vector.memset(zero_b[:], 0.0).then_inc(s_zero, 1)

            def degree_hots(i, first):
                for h in range(2):
                    c = i * (2 * FEED) + h * FEED
                    if not first:
                        dve.wait_ge(s_degmm, i * 2 + (h - 1))
                    for hot_out, n, key in ((low_hot, P, low_b), (bkt_hot, NS, bkt_b)):
                        ins = nc.vector.tensor_tensor(
                            hot_out[:, h, :, :], iota_b[:, 0:n].rearrange("p (a n) -> p a n", a=1).to_broadcast([P, FEED, n]),
                            key[:, bass.ds(c, FEED)].rearrange("p (c a) -> p c a", a=1).to_broadcast([P, FEED, n]),
                            ALU.is_equal)
                    ins.then_inc(s_hots, 1)

            degree_hots(0, True)
            with dve.Fori(1, NCOL // (2 * FEED)) as i:
                degree_hots(i, False)
            dve.wait_ge(s_degmm, NCOL // FEED)
            nc.vector.tensor_scalar(deg[:], psD[:, 0:NS], 1.0, None, ALU.add).then_inc(s_degr, 1)
            dve.wait_ge(s_degroot, 1)
            v.link(nc.vector.reciprocal(dinv[:], root[:]))
            nc.vector.memset(big[:, 0:NS * MSG], 0.0).then_inc(s_add[0], 1)

            def keep_rows(k, base):
                dve.wait_ge(s_rows[k], 32)
                for g in range(GROUPS + 1):
                    T = P if g < GROUPS - 1 else TAIL
                    if g < GROUPS:
                        if g >= 1:
                            dve.wait_ge(s_rowT[k], g)
                        nc.vector.tensor_copy(rows_f[0:T, :], rows[0:T, g, :]).then_inc(s_rowf[k], 1)
                    if g >= 1:
                        T = P if g - 1 < GROUPS - 1 else TAIL
                        dve.wait_ge(s_rowT[k], g)
                        c = slice((g - 1) * P, (g - 1) * P + T)
                        nc.vector.tensor_tensor(key_l[:, c], psA[(g - 1) % 2][:, 0:T], base[:, c], ALU.subtract)
                        nc.vector.tensor_copy(partner[:, c], psA[(g - 1) % 2][:, P:P + T]).then_inc(s_rowk[k], 1)
                dve.wait_ge(s_rowk[k], GROUPS)

            keep_rows(0, base0)

            def one_hots(k, p, i, off):
                for j in range(GRP):
                    ins = nc.vector.tensor_scalar(hot[:, p, j, :], iota_n[:], key_l[:, bass.ds(i * TPI + (off * GRP + j), 1)],
                                                  None, ALU.is_equal)
                ins.then_inc(s_hot[k], 1)

            def add_parts(k, tile_b, width, p, i, off, after):
                dve.wait_ge(s_part[k], after + 1)
                for j in range(GRP):
                    b = dve.value_load(tile_b[0:1, bass.ds(i * TPI + (off * GRP + j), 1)], min_val=0, max_val=NB)
                    at = sums[:, bass.ds(b, 1), 0:width].rearrange("p a d -> p (a d)")
                    dve.wait_ge(s_add[k], after * GRP + (j + 1))
                    ins = nc.vector.tensor_tensor(at, at, psC[p][:, j * width:(j + 1) * width], ALU.add)
                    ins.then_inc(s_add[k], 1)

            def attention(i, first):
                for g in range(GPI):
                    p = g % 2
                    G0 = i * GPI + g
                    dve.wait_ge(s_q, G0 + 1)
                    dve.wait_ge(s_got[0][g], i * 64 + 64)
                    rows4 = got[:, g * GRP:(g + 1) * GRP, :]
                    nc.vector.tensor_tensor(prod, psB[p][:, 0:GRP * D].rearrange("p (t d) -> p t d", d=D),
                                            rows4[:, :, 0:D], ALU.mult).then_inc(s_prod, 1)
                    dve.wait_ge(s_prod, G0 + 1)
                    if not (first and g < 2):
                        dve.wait_ge(s_exp, G0 - 1)
                    nc.vector.tensor_reduce(score[:, p, :], prod.rearrange("p t (h d) -> p (t h) d", d=DH),
                                            AX.X, ALU.add).then_inc(s_red, 1)
                    dve.wait_ge(s_red, G0 + 1)
                    nc.vector.tensor_scalar(score[:, p, :], score[:, p, :], -CLIP, CLIP, ALU.max, ALU.min
                                            ).then_inc(s_score, 1)
                    if not (first and g == 0):
                        dve.wait_ge(s_part[0], G0)
                    one_hots(0, 1 - p, i, g + 1)
                    dve.wait_ge(s_exp, G0 + 1)
                    nc.vector.tensor_tensor(
                        msg[:, p, :, 0:D].rearrange("p t (h d) -> p t h d", h=HEADS),
                        rows4[:, :, D:2 * D].rearrange("p t (h d) -> p t h d", h=HEADS),
                        msg[:, p, :, D:MSG].rearrange("p t (h a) -> p t h a", a=1).to_broadcast([P, GRP, HEADS, DH]),
                        ALU.mult).then_inc(s_msg, 1)
                    if not (first and g == 0):
                        add_parts(0, tile_b0, MSG, 1 - p, i, g - 1, G0 - 1)

            one_hots(0, 0, 0, 0)
            attention(0, True)
            with dve.Fori(1, ITERS) as i:
                attention(i, False)
            last = NT // GRP - 1
            add_parts(0, tile_b0, MSG, last % 2, ITERS - 1, GPI - 1, last)

            dve.wait_ge(s_add[0], NT + 1)
            weights = sums[:, :, D:MSG]
            v.link(nc.vector.tensor_scalar(weights, weights, 1e-8, None, ALU.add))
            v.link(nc.vector.reciprocal(weights, weights))
            v.link(nc.vector.tensor_tensor(
                T1[:, :, :].rearrange("p b (h d) -> p b h d", h=HEADS),
                sums[:, :, 0:D].rearrange("p b (h d) -> p b h d", h=HEADS),
                weights.rearrange("p b (h a) -> p b h a", a=1).to_broadcast([P, NS, HEADS, DH]), ALU.mult))
            v.link(nc.vector.tensor_tensor(T1[:, :, :], T1[:, :, :], Hf, ALU.add))
            v.link(nc.vector.tensor_tensor(Xf, Xf, T1[:, :, :], ALU.add))
            layer_norm(1)
            project(1)
            nc.vector.memset(big[:, 0:NS * MSG], 0.0).then_inc(s_add[1], 1)
            keep_rows(1, base1)

            def convolve(i, first):
                for g in range(GPI):
                    p = g % 2
                    G0 = i * GPI + g
                    if not (first and g < 2):
                        dve.wait_ge(s_part[1], G0 - 1)
                    one_hots(1, p, i, g)
                    if not (first and g == 0):
                        add_parts(1, tile_b1, D, 1 - p, i, g - 1, G0 - 1)

            convolve(0, True)
            with dve.Fori(1, ITERS) as i:
                convolve(i, False)
            add_parts(1, tile_b1, D, last % 2, ITERS - 1, GPI - 1, last)

            dve.wait_ge(s_add[1], NT + 1)
            T = T1[:, :, :]
            v.link(nc.vector.tensor_tensor(T, sums[:, :, 0:D], G, ALU.add))
            v.link(nc.vector.tensor_tensor(T, T, wide(dinv), ALU.mult))
            v.link(nc.vector.tensor_tensor(T, T, Q[:, :, :], ALU.add))
            for n in range(2):
                v.link(nc.vector.tensor_tensor(T, T, bias2[:, n:n + 1, :].to_broadcast([P, NS, D]), ALU.add))
            nc.vector.tensor_scalar(G, T, 20.0, None, ALU.min).then_inc(s_y, 1)
            dve.wait_ge(s_ye, 1)
            v.link(nc.vector.scalar_tensor_tensor(out=Hf, in0=Hf, scalar=2.0, in1=Hf, op0=ALU.add, op1=ALU.mult))
            v.link(nc.vector.tensor_scalar(G, Hf, 2.0, None, ALU.add))
            v.link(nc.vector.reciprocal(G, G))
            v.link(nc.vector.tensor_tensor(Hf, Hf, G, ALU.mult))
            v.link(nc.vector.tensor_tensor(T, T, Hf, ALU.mult))
            nc.vector.tensor_tensor(T, T, Xf, ALU.add).then_inc(s_fin, 1)


_INS = ["x", "src", "dst", "L0_gnn_qW", "L0_gnn_kW", "L0_gnn_vW", "L1_gnn_W_gcn", "L1_gnn_b_gcn",
        "L1_gnn_W_lin", "L1_gnn_b_lin"]


def kernel(**inputs):
    import numpy as _np
    import concourse.bacc as _bacc
    from concourse import mybir as _mybir
    from concourse.bass_utils import run_bass_kernel_spmd as _run

    nc = _bacc.Bacc("TRN2", target_bir_lowering=False, num_devices=1)
    arrays, args = {}, []
    for name in _INS:
        a = _np.ascontiguousarray(inputs[name])
        arrays[f"in_{name}"] = a
        args.append(nc.dram_tensor(f"in_{name}", a.shape, _mybir.dt.from_np(a.dtype), kind="ExternalInput").ap())
    args.append(nc.dram_tensor("out_x", inputs["x"].shape, _mybir.dt.float32, kind="ExternalOutput").ap())
    gnn_kernel(nc, *args)
    r = _run(nc, [arrays], core_ids=[0])
    return r.results[0]["out_x"]
```

```python
from contextlib import ExitStack

import concourse.bass as bass
from concourse import mybir

ALU = mybir.AluOpType
ACT = mybir.ActivationFunctionType
AX = mybir.AxisListType
F32 = mybir.dt.float32
BF16 = mybir.dt.bfloat16
I32 = mybir.dt.int32
U8 = mybir.dt.uint8

P = 128
HEADS = 4
EPS = 1e-5
CLIP = 10.0
GRP = 4
GPI = 4
TPI = GRP * GPI
PARTNER_BITS, LOW_BITS, BUCKET_AT, NORMAL_BIT = 13, 7, 21, 27


class Chain:

    def __init__(self, eng, sem):
        self.eng, self.sem, self.n = eng, sem, 0

    def __call__(self, ins):
        ins.then_inc(self.sem, 1)
        self.n += 1

    def wait(self, but=0):
        if self.n > but:
            self.eng.wait_ge(self.sem, self.n - but)

    def link(self, ins):
        self(ins)
        self.wait()


def gnn_kernel(nc, x, src, dst, qW, kW, vW, W_gcn, b_gcn, W_lin, b_lin, out):
    N, D = x.shape
    E = src.shape[0]
    DH = D // HEADS
    MSG = D + HEADS
    NB = -(-N // P)
    NS = NB + 1
    FULL = N // P
    REST = N - FULL * P
    NCOL = -(-E // (P * TPI)) * TPI
    LAST = E - (P - 1) * NCOL
    PAD_KEY = NB * P
    NT = -(-((E + NB * (P - 1)) // P) // TPI) * TPI
    NTP = NT + TPI
    LIST_TILES = E // P + NB + 2
    GROUPS = NT // P + 1
    TAIL = NT - (GROUPS - 1) * P
    HT = NTP // 2
    HIGHEST_START = (LIST_TILES - 1) * P
    ITERS = NT // TPI
    LANE = 1024
    HALF = LANE // 2
    IN_LANE = LANE.bit_length() - 1
    ACROSS = P.bit_length() - 1
    TURNS = HALF // P
    NEVER = (1 << NORMAL_BIT) | (NB << BUCKET_AT) | (1 << (PARTNER_BITS + LOW_BITS))
    assert 0 < LAST <= NCOL and HT <= 512 and 0 < TAIL < P and NCOL <= NT
    assert NCOL + NB <= LANE and NT <= LANE and NS * P <= 1 << PARTNER_BITS and NS < 64
    assert E + P * (NT - -(-E // P)) <= LIST_TILES * P + P * 2 and P * NCOL <= LIST_TILES * P
    BACK = P * NCOL // LANE

    ctx = ExitStack()
    with ctx:
        def sb(name, shape, dt=F32):
            return ctx.enter_context(nc.sbuf_tensor(name, shape, dt))

        def ps(name):
            return ctx.enter_context(nc.psum_tensor(name, [P, 512], F32))

        def sem(name):
            return ctx.enter_context(nc.semaphore(name))

        kv_table = nc.dram_tensor("kv_table", [NS * P, 2 * D], F32, kind="Internal").ap()
        g_table = nc.dram_tensor("g_table", [NS * P, D], F32, kind="Internal").ap()
        list1 = nc.dram_tensor("list1", [LIST_TILES * P, 2], I32, kind="Internal").ap()
        sorted1 = nc.dram_tensor("sorted1", [NT * P, 2], I32, kind="Internal").ap()

        X = sb("X", [P, NS, D])
        H = sb("H", [P, NS, D])
        Q = sb("Q", [P, NS, D])
        T1 = sb("T1", [P, NS, D])
        sums = sb("sums", [P, NS, MSG])
        G = sb("G", [P, NS, D])
        gf = G[:, :, :].rearrange("p b d -> p (b d)")
        back_pair = gf[:, 0:2 * LANE].bitcast(I32).rearrange("p (c k) -> p c k", k=2)
        nxt_i = gf[:, 2 * LANE:2 * LANE + NCOL].bitcast(I32)
        sign_out = gf[:, 2 * LANE + NCOL:2 * LANE + 2 * NCOL].bitcast(BF16).rearrange("p (k c) -> p k c", k=2)

        src_i = sb("src_i", [P, NCOL], I32)
        dst_i = sb("dst_i", [P, NCOL], I32)
        bkt_b = sb("bkt_b", [P, NT], BF16)
        low_b = sb("low_b", [P, NT], BF16)
        pair1 = sb("pair1", [P, NCOL, 2], I32)

        t1f = T1[:, :, :].rearrange("p b d -> p (b d)")
        keys = [t1f[:, n * LANE:(n + 1) * LANE] for n in range(2)]
        plain = t1f[:, 2 * LANE:3 * LANE]
        pads_i = sb("pads_i", [P, NB], I32)
        pad_on = sb("pad_on", [P, NB], I32)
        lane_i = sb("lane_i", [P, NB], I32)
        signs = sb("signs", [P, ACROSS + 1])
        sign_i = sb("sign_i", [P, ACROSS + 1], I32)
        bounds = sb("bounds", [P, NB])
        over = sb("over", [P, 2, NB])

        rows = sb("rows", [P, GROUPS, 2 * P], I32)
        rows_f = sb("rows_f", [P, 2 * P])
        key_l = sb("key_l", [P, NTP])
        partner = sb("partner", [P, NTP], I32)
        base1 = sb("base1", [P, NTP])
        packed = sb("packed", [P, NT], I32)
        tile_b0 = sb("tile_b0", [1, NTP], I32)
        tile_b1 = sb("tile_b1", [1, NTP], I32)
        tile_s1 = sb("tile_s1", [1, NTP], I32)
        sums_flat = sums[:, :, :].rearrange("p b m -> p (b m)")
        iota_t = sums_flat[:, 0:NTP]
        begun = sums_flat[:, NTP:2 * NTP]

        iota_n = sb("iota_n", [P, P])
        iota_b = sb("iota_b", [P, P], BF16)
        diff = sb("diff", [P, P])
        ident = sb("ident", [P, P])
        ones = sb("ones", [P, P])
        zero_b = sb("zero_b", [P, P], BF16)
        qkv_w = sb("qkv_w", [D, 3 * D])
        gl_w = sb("gl_w", [D, 2 * D])
        bias2 = sb("bias2", [P, 2, D])

        above = sb("above", [P, NS + 1])
        n_all = sb("n_all", [P, NS])
        n_tile = sb("n_tile", [P, NS])
        n_tile_i = sb("n_tile_i", [P, NS], I32)
        tile_end = sb("tile_end", [P, NS])
        excess = sb("excess", [P, NS])
        cols = sb("cols", [NS, 2])
        mark = sb("mark", [1, 1])
        need = sb("need", [P, NB])
        flag = sb("flag", [P, 2])
        flag_i = sb("flag_i", [1, 1], I32)
        mean = sb("mean", [P, NS])
        var = sb("var", [P, NS])
        rstd = sb("rstd", [P, NS])
        deg = sb("deg", [P, NS])
        root = sb("root", [P, NS])
        dinv = sb("dinv", [P, NS])

        stage = sb("stage", [P, 2, D])
        hT = sb("hT", [D, 2, P])
        kv_stage = sb("kv_stage", [P, 2, 2 * D])
        got = sb("got", [P, TPI, 2 * D])
        low_hot = sb("low_hot", [P, GRP, P], BF16)
        bkt_hot = sb("bkt_hot", [P, GRP, NS], BF16)
        gotf = got[:, :, :].rearrange("p t w -> p (t w)")
        turned = [gotf[:, n * LANE:(n + 1) * LANE].rearrange("p (h c) -> p h c", h=2) for n in range(2)]
        idx_ring = sb("idx_ring", [P, TPI], I32)
        hot = sb("hot", [P, 4, GRP, P])
        hotT = sb("hotT", [P, 2, GRP * P])
        prod = sb("prod", [P, GRP, D])
        score = sb("score", [P, 2, GRP * HEADS])
        msg = sb("msg", [P, 2, GRP, MSG])

        psA = [ps("psA0"), ps("psA1")]
        psB = [ps("psB0"), ps("psB1")]
        psC = [ps("psC0"), ps("psC1")]
        psD = ps("psD")
        psE = ps("psE")

        s_edges = sem("edges_loaded")
        s_x = sem("x_loaded")
        s_w = sem("weights_loaded")
        s_pads = sem("pads_set")
        s_iota = sem("iota_made")
        s_fill = sem("lists_filled")
        s_const = sem("constants_made")
        s_a = sem("counts_made")
        s_above = sem("counts_on_pe")
        s_cols = sem("rows_for_columns")
        s_colT = sem("columns_turned")
        s_begun = sem("begun_made")
        s_tile = sem("tile_data_on_pe")
        s_tiled = sem("tile_data_kept")
        s_vf = sem("vector_chain_unsorted")
        s_h = [sem("activations0"), sem("activations1")]
        s_g = sem("self_terms")
        s_v = sem("vector_chain")
        s_flagp = sem("disorder_counted")
        s_flagd = sem("disorder_marked")
        s_flag = sem("flag_made")
        s_bkt = sem("buckets_made")
        s_chain = [sem("sort_chain1"), sem("sort_chain0")]
        s_lane = [[sem(f"lane_done{k}{h}") for h in range(2)] for k in range(2)]
        s_plain = [[sem(f"signs_off{k}{h}") for h in range(2)] for k in range(2)]
        s_turn = [[sem(f"sort_turned{k}{h}") for h in range(2)] for k in range(2)]
        s_cross = [[sem(f"cross_done{k}{h}") for h in range(2)] for k in range(2)]
        s_back = [[sem(f"sort_back{k}{h}") for h in range(2)] for k in range(2)]
        s_signed = [[sem(f"signs_on{k}{h}") for h in range(2)] for k in range(2)]
        s_final = sem("sorted_turned")
        s_packed = sem("sorted_kept")
        s_pair = sem("pairs_made")
        s_list1 = sem("list1_written")
        s_var = [sem("variance0"), sem("variance1")]
        s_root = [sem("root0"), sem("root1")]
        s_degr = sem("degree_plus_one")
        s_degroot = sem("degree_root")
        s_dinv = sem("degree_inverse_root")
        s_pstage = [sem("p_staged0"), sem("p_staged1")]
        s_pT = [sem("p_turned0"), sem("p_turned1")]
        s_phT = [sem("p_kept0"), sem("p_kept1")]
        s_pmm = [sem("p_product0"), sem("p_product1")]
        s_pq = [sem("p_first_out0"), sem("p_first_out1")]
        s_pkv = [sem("p_second_out0"), sem("p_second_out1")]
        s_tab = [[sem("table0_a"), sem("table0_b")], [sem("table1_a"), sem("table1_b")]]
        s_hots = sem("degree_hots")
        s_degmm = sem("degree_products")
        s_rows = sem("rows_loaded")
        s_rowf = sem("rows_float")
        s_rowT = sem("rows_turned")
        s_rowk = sem("rows_kept")
        s_edge0 = sem("edges0_unpacked")
        s_align = sem("tile_rows_written")
        s_zero = sem("degree_zeroed")
        s_add = [sem("tiles_added0"), sem("tiles_added1")]
        s_idx = [sem("indices0"), sem("indices1")]
        s_got = [[sem(f"gathered{k}_{g}") for g in range(GPI)] for k in range(2)]
        s_hot = [sem("hot0"), sem("hot1")]
        s_hotp = sem("hot_turned")
        s_hotT = sem("hot_turned_kept")
        s_q = sem("queries_of_edges")
        s_prod = sem("query_key_products")
        s_red = sem("scores_summed")
        s_score = sem("scores_clipped")
        s_exp = sem("exponentials")
        s_msg = sem("messages_made")
        s_part = [sem("bucket_parts0"), sem("bucket_parts1")]
        s_y = sem("final_exp_in")
        s_ye = sem("final_exp_out")
        s_fin = sem("result_made")
        s_out = sem("result_stored")
        s_pool = sem("pool_waited")

        def per_p(flat, n=NCOL):
            return flat.rearrange("(p c) -> p c", c=n)

        block = ctx.enter_context(nc.Block())

        @block.sync
        def _(sp):
            sp.wait_ge(s_pads, 1)
            body = (P - 1) * NCOL
            sp.dma_start(src_i[0:P - 1, :], per_p(src[0:body])).then_inc(s_edges, 16)
            sp.dma_start(src_i[P - 1:P, 0:LAST], src[body:E].rearrange("(p c) -> p c", p=1)).then_inc(s_edges, 16)
            sp.dma_start(dst_i[0:P - 1, :], per_p(dst[0:body])).then_inc(s_edges, 16)
            sp.dma_start(dst_i[P - 1:P, 0:LAST], dst[body:E].rearrange("(p c) -> p c", p=1)).then_inc(s_edges, 16)
            sp.dma_start(nxt_i[0:P - 1, :], per_p(dst[1:body + 1])).then_inc(s_edges, 16)
            sp.dma_start(nxt_i[P - 1:P, 0:LAST - 1], dst[body + 1:E].rearrange("(p c) -> p c", p=1)).then_inc(s_edges, 16)
            flat_rows = rows[:, :, :].rearrange("p g c -> p (g c)")
            sp.dma_start(list1.rearrange("(p s) c -> p (s c)", p=P),
                         flat_rows[:, 0:2 * LIST_TILES]).then_inc(s_fill, 16)

            sp.wait_ge(s_list1, 16)
            sp.wait_ge(s_tiled, 1)
            sorted1_rows = sorted1.rearrange("(t l) c -> t (l c)", l=P)
            list1_flat = list1.rearrange("s c -> (s c)").rearrange("(a f) -> a f", a=1)
            with sp.Fori(0, NT) as t:
                start = sp.value_load(tile_s1[0:1, bass.ds(t, 1)], min_val=0, max_val=HIGHEST_START)
                sp.dma_start(sorted1_rows[bass.ds(t, 1), :],
                             list1_flat[:, bass.ds(start * 2, 2 * P)]).then_inc(s_align, 16)
            sp.wait_ge(s_align, 16 * NT)
            head = (GROUPS - 1) * P
            sp.dma_start(rows[:, 0:GROUPS - 1, :],
                         sorted1[0:head * P, :].rearrange("(g t l) c -> t g (l c)", t=P, l=P)).then_inc(s_rows, 16)
            sp.dma_start(rows[0:TAIL, GROUPS - 1, :],
                         sorted1[head * P:NT * P, :].rearrange("(t l) c -> t (l c)", l=P)).then_inc(s_rows, 16)

            sp.wait_ge(s_fin, 1)
            sp.dma_start(out[0:FULL * P, :].rearrange("(b p) d -> p b d", p=P), T1[:, 0:FULL, :]).then_inc(s_out, 16)
            sp.dma_start(out[FULL * P:N, :], T1[0:REST, FULL, :]).then_inc(s_out, 16)
            sp.wait_ge(s_out, 32)

        @block.gpsimd
        def _(pool):
            nc.gpsimd.iota(iota_t, [[1, NTP]], base=0, channel_multiplier=0,
                           allow_small_or_imprecise_dtypes=True).then_inc(s_iota, 1)
            nc.gpsimd.iota(iota_n[:], [[1, P]], base=0, channel_multiplier=0,
                           allow_small_or_imprecise_dtypes=True).then_inc(s_iota, 1)
            nc.gpsimd.iota(diff[:], [[1, P]], base=0, channel_multiplier=-1,
                           allow_small_or_imprecise_dtypes=True).then_inc(s_iota, 1)
            nc.gpsimd.iota(pads_i[:], [[1, NB]], base=0, channel_multiplier=0).then_inc(s_iota, 1)
            nc.gpsimd.iota(lane_i[:], [[0, NB]], base=0, channel_multiplier=1).then_inc(s_iota, 1)

            def gathers(k, table, width, free):
                def one(i, first):
                    for g in range(GPI):
                        if g % 2 == 0:
                            pool.wait_ge(s_idx[k], i * 2 + (g // 2 + 1))
                        if not first:
                            pool.wait_ge(free, i * GPI + (g + 1 - GPI))
                        pool.sem_inc(s_pool, 1)
                        for j in range(GRP):
                            n = g * GRP + j
                            nc.gpsimd.indirect_dma_start(
                                out=got[:, n, 0:width], out_offset=None, in_=table,
                                in_offset=bass.IndirectOffsetOnAxis(ap=idx_ring[:, n:n + 1], axis=0)).then_inc(s_got[k][g], 16)
                one(0, True)
                with pool.Fori(1, ITERS) as i:
                    one(i, False)

            for h in range(2):
                pool.wait_ge(s_tab[0][h], 16 * (NS // 2))
            gathers(0, kv_table, 2 * D, s_msg)
            for h in range(2):
                pool.wait_ge(s_tab[1][h], 16 * (NS // 2))
            gathers(1, g_table, D, s_part[1])

        @block.scalar
        def _(act):
            a = Chain(act, s_a)

            act.wait_ge(s_pads, 1)
            act.dma_start(X[:, 0:FULL, :], x[0:FULL * P, :].rearrange("(b p) d -> p b d", p=P)).then_inc(s_x, 16)
            act.dma_start(X[0:REST, FULL, :], x[FULL * P:N, :]).then_inc(s_x, 16)
            for n, w in enumerate((qW, kW, vW)):
                act.dma_start(qkv_w[:, n * D:(n + 1) * D], w).then_inc(s_w, 16)
            for n, w in enumerate((W_gcn, W_lin)):
                act.dma_start(gl_w[:, n * D:(n + 1) * D], w).then_inc(s_w, 16)
            for n, b in enumerate((b_gcn, b_lin)):
                act.dma_start(bias2[:, n, :], b.rearrange("(a d) -> a d", a=1).to_broadcast([P, D])).then_inc(s_w, 16)

            def root_of(k):
                act.wait_ge(s_var[k], 1)
                nc.scalar.activation(rstd[:], var[:], ACT.Sqrt).then_inc(s_root[k], 1)

            def count_above(k, key_i, buckets):
                for b in buckets:
                    a.wait(1)
                    a(nc.scalar.activation(sign_out[:, b % 2, :], key_i[:], ACT.Sign, bias=bounds[:, b:b + 1],
                                           accum_out=over[:, k, b:b + 1]))

            def sort_turns(k):
                for s in range(ACROSS):
                    for h in range(2):
                        cut = slice(h * HALF, (h + 1) * HALF)
                        act.wait_ge(s_lane[k][h], s + 1)
                        nc.scalar.activation(plain[:, cut], keys[0][:, cut], ACT.Copy,
                                             scale=signs[:, s:s + 1]).then_inc(s_plain[k][h], 1)
                    for h in range(2):
                        cut = slice(h * HALF, (h + 1) * HALF)
                        act.wait_ge(s_back[k][h], s + 1)
                        nc.scalar.activation(keys[0][:, cut], psB[h][:, :], ACT.Copy,
                                             scale=signs[:, s + 1:s + 2]).then_inc(s_signed[k][h], 1)

            def project(k, table):
                def one(i, first):
                    for h in range(2):
                        b = i * 2 + h
                        if not first:
                            act.wait_ge(s_pT[k], i * 2 + (h - 1))
                        nc.scalar.copy(stage[:, h, :], H[:, bass.ds(b, 1), :].rearrange("p a d -> p (a d)")
                                       ).then_inc(s_pstage[k], 1)
                    for h in range(2):
                        act.wait_ge(s_pT[k], i * 2 + (h + 1))
                        nc.scalar.copy(hT[:, h, :], psA[h][0:D, 0:P]).then_inc(s_phT[k], 1)
                    for h in range(2):
                        b = i * 2 + h
                        act.wait_ge(s_pmm[k], i * 2 + (h + 1))
                        w = D if k else 2 * D
                        nc.scalar.copy(Q[:, bass.ds(b, 1), :].rearrange("p a d -> p (a d)"),
                                       psB[h][:, D:2 * D] if k else psB[h][:, 0:D]).then_inc(s_pq[k], 1)
                        if not first:
                            act.wait_ge(s_tab[k][h], i * 16)
                        if k == 0:
                            nc.scalar.copy(kv_stage[:, h, :], psB[h][:, D:3 * D]).then_inc(s_pkv[k], 1)
                        else:
                            nc.scalar.activation(kv_stage[:, h, 0:D], psB[h][:, 0:D], ACT.Copy,
                                                 scale=dinv[:, bass.ds(b, 1)]).then_inc(s_pkv[k], 1)
                        act.wait_ge(s_pkv[k], i * 2 + (h + 1))
                        if k == 1:
                            nc.scalar.copy(G[:, bass.ds(b, 1), :].rearrange("p a d -> p (a d)"),
                                           kv_stage[:, h, 0:D]).then_inc(s_g, 1)
                        act.dma_start(table.rearrange("(b p) w -> b p w", p=P)[bass.ds(b, 1), :, :].rearrange("a p w -> (a p) w"),
                                      kv_stage[:, h, 0:w]).then_inc(s_tab[k][h], 16)
                act.wait_ge(s_h[k], 1)
                one(0, True)
                with act.Fori(1, NS // 2) as i:
                    one(i, False)

            def feed_half(k, i, h):
                nc.scalar.copy(idx_ring[:, h * 8:h * 8 + 8], partner[:, bass.ds(i * TPI + h * 8, 8)]).then_inc(s_idx[k], 1)

            act.wait_ge(s_const, 1)
            act.wait_ge(s_edges, 16 * 6)
            count_above(0, src_i, range(NB // 2))
            root_of(0)
            count_above(0, src_i, range(NB // 2, NB))

            act.wait_ge(s_flag, 1)
            act.wait_ge(s_fill, 16)
            unsorted = act.value_load(flag_i[0:1, 0:1], min_val=0, max_val=1)
            with act.If(unsorted > 0):
                sort_turns(0)
                act.wait_ge(s_pair, 2)
                act.dma_start(list1[0:BACK * LANE, :].rearrange("(p c) k -> p (c k)", p=BACK),
                              back_pair[0:BACK, :, :].rearrange("p c k -> p (c k)")).then_inc(s_list1, 16)
            with act.Else():
                act.wait_ge(s_pair, 1)
                act.dma_start(list1[0:P * NCOL, :].rearrange("(p c) k -> p (c k)", p=P),
                              pair1[:, :, :].rearrange("p c k -> p (c k)")).then_inc(s_list1, 16)
            project(0, kv_table)
            count_above(1, dst_i, range(NB))
            sort_turns(1)
            for h in range(2):
                act.wait_ge(s_final, h + 1)
                rows_used = NT // (2 * TURNS)
                nc.scalar.copy(
                    packed[:].bitcast(F32).rearrange("l (p n) -> l p n", n=2 * TURNS)[:, :, h * TURNS:(h + 1) * TURNS],
                    psA[h][:, :].rearrange("l (p n) -> l p n", n=TURNS)[:, 0:rows_used, :]).then_inc(s_packed, 1)

            act.wait_ge(s_edge0, 1)
            feed_half(0, 0, 0)
            feed_half(0, 0, 1)

            def attention(i, first):
                for g in range(GPI):
                    p = g % 2
                    G0 = i * GPI + g
                    act.wait_ge(s_score, G0 + 1)
                    if not (first and g < 2):
                        act.wait_ge(s_part[0], G0 - 1)
                    nc.scalar.activation(msg[:, p, :, D:MSG],
                                         score[:, p, :].rearrange("p (t h) -> p t h", h=HEADS),
                                         ACT.Exp).then_inc(s_exp, 1)
                    act.wait_ge(s_hotp, G0 + 3)
                    act.wait_ge(s_q, G0 + 1)
                    nc.scalar.copy(hotT[:, p, :], psA[p][:, :]).then_inc(s_hotT, 1)
                    if p == 1:
                        act.wait_ge(s_got[0][g - 1], i * 64 + 64)
                        act.wait_ge(s_got[0][g], i * 64 + 64)
                        feed_half(0, i + 1, g // 2)

            for n in range(2):
                act.wait_ge(s_hotp, n + 1)
                nc.scalar.copy(hotT[:, n, :], psA[n][:, :]).then_inc(s_hotT, 1)
            attention(0, True)
            with act.Fori(1, ITERS) as i:
                attention(i, False)

            root_of(1)
            act.wait_ge(s_degr, 1)
            nc.scalar.activation(root[:], deg[:], ACT.Sqrt).then_inc(s_degroot, 1)
            act.wait_ge(s_dinv, 1)
            project(1, g_table)

            act.wait_ge(s_rowk, GROUPS)
            feed_half(1, 0, 0)
            feed_half(1, 0, 1)
            with act.Fori(0, ITERS) as i:
                for h in range(2):
                    act.wait_ge(s_got[1][2 * h], i * 64 + 64)
                    act.wait_ge(s_got[1][2 * h + 1], i * 64 + 64)
                    feed_half(1, i + 1, h)

            act.wait_ge(s_y, 1)
            nc.scalar.activation(H[:, :, :], G[:, :, :], ACT.Exp).then_inc(s_ye, 1)

        @block.tensor
        def _(pe):
            pe.wait_ge(s_const, 1)

            def above_bounds(k):
                pe.wait_ge(s_a, (k + 1) * NB)
                nc.tensor.matmul((psE if k else psC[0])[:, 0:NB], ones[:], over[:, k, :], start=True, stop=True).then_inc(s_above, 1)

            def sort_turns(k):
                for s in range(ACROSS):
                    for h in range(2):
                        pe.wait_ge(s_plain[k][h], s + 1)
                        for n in range(TURNS):
                            c = h * HALF + n * P
                            mm = nc.tensor.transpose(psA[h][:, n:P * TURNS:TURNS], plain[:, c:c + P], ident[:])
                        mm.then_inc(s_turn[k][h], 1)
                    for h in range(2):
                        pe.wait_ge(s_cross[k][h], s + 1)
                        for n in range(TURNS):
                            mm = nc.tensor.transpose(psB[h][:, n * P:(n + 1) * P], turned[0][:, h, n:P * TURNS:TURNS],
                                                     ident[:])
                        mm.then_inc(s_back[k][h], 1)

            above_bounds(0)
            pe.wait_ge(s_flagd, 1)
            nc.tensor.matmul(psD[:, 0:1], ones[:], flag[:, 0:1], start=True, stop=True).then_inc(s_flagp, 1)
            pe.wait_ge(s_flag, 1)
            unsorted = pe.value_load(flag_i[0:1, 0:1], min_val=0, max_val=1)
            with pe.If(unsorted > 0):
                sort_turns(0)
            with pe.Else():
                pe.wait_ge(s_flag, 1)

            def project(k, weights, width):
                def one(i, first):
                    for h in range(2):
                        pe.wait_ge(s_pstage[k], i * 2 + (h + 1))
                        if not first:
                            pe.wait_ge(s_phT[k], i * 2 + (h - 1))
                        nc.tensor.transpose(psA[h][0:D, 0:P], stage[:, h, :], ident[:]).then_inc(s_pT[k], 1)
                        pe.wait_ge(s_phT[k], i * 2 + (h + 1))
                        if not first:
                            pe.wait_ge(s_pkv[k], i * 2 + (h - 1))
                        nc.tensor.matmul(psB[h][:, 0:width], hT[:, h, :], weights[:, 0:width],
                                         start=True, stop=True).then_inc(s_pmm[k], 1)
                one(0, True)
                with pe.Fori(1, NS // 2) as i:
                    one(i, False)

            pe.wait_ge(s_w, 16 * 7)
            project(0, qkv_w, 3 * D)

            above_bounds(1)
            sort_turns(1)
            for h in range(2):
                pe.wait_ge(s_lane[1][h], ACROSS + 1)
                for n in range(TURNS):
                    c = h * HALF + n * P
                    mm = nc.tensor.transpose(psA[h][:, n:P * TURNS:TURNS], keys[0][:, c:c + P], ident[:])
                mm.then_inc(s_final, 1)

            pe.wait_ge(s_cols, 1)
            nc.tensor.transpose(psE[0:NS, 128:256], tile_end[:], ident[:])
            nc.tensor.transpose(psE[0:NS, 256:384], excess[:], ident[:]).then_inc(s_colT, 1)
            pe.wait_ge(s_begun, 1)
            for m in range(2):
                nc.tensor.matmul(psC[m][:, 0:HT], ones[0:NB, :], begun[0:NB, m * HT:(m + 1) * HT],
                                 start=True, stop=True)
                mm = nc.tensor.matmul((psE if m else psD)[0:1, 0:HT], cols[0:NB, 1:2],
                                      begun[0:NB, m * HT:(m + 1) * HT], start=True, stop=True)
            mm.then_inc(s_tile, 1)

            def turn_hot(g, G0):
                pe.wait_ge(s_hot[0], G0 + 1)
                for j in range(GRP):
                    mm = nc.tensor.transpose(psA[g % 2][:, j * P:(j + 1) * P], hot[:, g, j, :], ident[:])
                mm.then_inc(s_hotp, 1)

            def queries(p, i, off, G0):
                pe.wait_ge(s_hotT, G0 + 1)
                for j in range(GRP):
                    b = pe.value_load(tile_b0[0:1, bass.ds(i * TPI + (off * GRP + j), 1)], min_val=0, max_val=NB)
                    mm = nc.tensor.matmul(psB[p][:, j * D:(j + 1) * D], hotT[:, p, j * P:(j + 1) * P],
                                          Q[:, bass.ds(b, 1), :].rearrange("p a d -> p (a d)"), start=True, stop=True)
                mm.then_inc(s_q, 1)

            def attention(i, first):
                for g in range(GPI):
                    p = g % 2
                    G0 = i * GPI + g
                    if not (first and g == 0):
                        pe.wait_ge(s_prod, G0)
                    queries(1 - p, i, g + 1, G0 + 1)
                    pe.wait_ge(s_hotT, G0 + 1)
                    turn_hot((g + 2) % 4, G0 + 2)
                    pe.wait_ge(s_hots, G0 + 1)
                    for j in range(GRP):
                        mm = nc.tensor.matmul(psD[:, 0:NS], low_hot[:, j, :], bkt_hot[:, j, :],
                                              start=False, stop=False, skip_group_check=True)
                    mm.then_inc(s_degmm, 1)
                    pe.wait_ge(s_msg, G0 + 1)
                    if not (first and g < 2):
                        pe.wait_ge(s_add[0], G0 * GRP + (1 - GRP))
                    for j in range(GRP):
                        mm = nc.tensor.matmul(psC[p][:, j * MSG:(j + 1) * MSG], hot[:, g, j, :], msg[:, p, j, :],
                                              start=True, stop=True)
                    mm.then_inc(s_part[0], 1)

            pe.wait_ge(s_tiled, 1)
            nc.tensor.matmul(psD[:, 0:NS], zero_b[:], zero_b[:, 0:NS], start=True, stop=False, skip_group_check=True)
            turn_hot(0, 0)
            turn_hot(1, 1)
            queries(0, 0, 0, 0)
            attention(0, True)
            with pe.Fori(1, ITERS) as i:
                attention(i, False)

            project(1, gl_w, 2 * D)
            for g in range(GROUPS):
                T = P if g < GROUPS - 1 else TAIL
                pe.wait_ge(s_rowf, g + 1)
                if g >= 2:
                    pe.wait_ge(s_rowk, g - 1)
                nc.tensor.transpose(psA[g % 2][:, 0:T], rows_f[0:T, 0:2 * P:2], ident[0:T, 0:T])
                nc.tensor.transpose(psA[g % 2][:, P:P + T], rows_f[0:T, 1:2 * P:2],
                                    ident[0:T, 0:T]).then_inc(s_rowT, 1)

            def convolve(i, first):
                for g in range(GPI):
                    p = g % 2
                    G0 = i * GPI + g
                    pe.wait_ge(s_hot[1], G0 + 1)
                    pe.wait_ge(s_got[1][g], i * 64 + 64)
                    if not (first and g < 2):
                        pe.wait_ge(s_add[1], G0 * GRP + (1 - GRP))
                    for j in range(GRP):
                        mm = nc.tensor.matmul(psC[p][:, j * D:(j + 1) * D], hot[:, g, j, :],
                                              got[:, g * GRP + j, 0:D], start=True, stop=True)
                    mm.then_inc(s_part[1], 1)

            convolve(0, True)
            with pe.Fori(1, ITERS) as i:
                convolve(i, False)

        @block.vector
        def _(dve):
            v = Chain(dve, s_v)

            for t in (src_i[:], dst_i[:], nxt_i):
                nc.vector.memset(t, PAD_KEY)
            nc.vector.memset(X[:, FULL:NS, :], 0.0)
            all_rows = rows[:, :, :].rearrange("p g (l c) -> p (g l) c", c=2)
            nc.vector.memset(all_rows[:, :, 0], PAD_KEY)
            nc.vector.memset(all_rows[:, :, 1], 0)
            nc.vector.memset(ones[:], 1.0)
            nc.vector.memset(zero_b[:], 0.0).then_inc(s_pads, 1)
            nc.vector.memset(bkt_b[:, NCOL:NT], 63.0)
            v.link(nc.vector.memset(low_b[:, NCOL:NT], 255.0))
            dve.wait_ge(s_iota, 5)
            nc.vector.tensor_scalar(ident[:], diff[:], 0.0, None, ALU.is_equal)
            nc.vector.tensor_copy(iota_b[:], iota_n[:])
            for lev in range(ACROSS + 1):
                nc.vector.tensor_scalar(sign_i[:, lev:lev + 1], lane_i[:, 0:1], lev, 1, ALU.arith_shift_right, ALU.bitwise_and)
            v.link(nc.vector.tensor_scalar(pads_i[:], pads_i[:], BUCKET_AT, NEVER & ~(63 << BUCKET_AT),
                                           ALU.logical_shift_left, ALU.bitwise_or))
            v.link(nc.vector.tensor_scalar(signs[:], sign_i[:], 2.0, -1.0, ALU.mult, ALU.add))
            v.link(nc.vector.memset(signs[:, ACROSS:ACROSS + 1], 1.0))
            nc.vector.tensor_scalar(bounds[:], iota_n[:, 0:NB], -float(P), 0.5 - P, ALU.mult, ALU.add).then_inc(s_const, 1)
            dve.wait_ge(s_const, 1)

            def pack(key, partner_of):
                ki = keys[0].bitcast(I32)
                kj = keys[1].bitcast(I32)
                v.link(nc.vector.memset(ki[:, NCOL:LANE], NEVER))
                v.link(nc.vector.tensor_scalar(kj[:, 0:NCOL], key[:], LOW_BITS, BUCKET_AT,
                                               ALU.logical_shift_right, ALU.logical_shift_left))
                v.link(nc.vector.tensor_scalar(ki[:, 0:NCOL], key[:], P - 1, PARTNER_BITS,
                                               ALU.bitwise_and, ALU.logical_shift_left))
                v.link(nc.vector.tensor_tensor(kj[:, 0:NCOL], kj[:, 0:NCOL], partner_of[:], ALU.bitwise_or))
                v.link(nc.vector.tensor_tensor(ki[:, 0:NCOL], ki[:, 0:NCOL], kj[:, 0:NCOL], ALU.bitwise_or))
                v.link(nc.vector.tensor_scalar(ki[:, 0:NCOL], ki[:, 0:NCOL], 1 << NORMAL_BIT, None, ALU.bitwise_or))

            def sort(k):
                c = Chain(dve, s_chain[k])
                at = 0

                def order(src_ap, dst_ap, k_, outer, descending, after, upper=None):
                    if after:
                        dve.wait_ge(s_chain[k], after)
                    if descending is None:
                        a = [t.rearrange("p (g two k) -> p g two k", two=2, k=k_)
                             for t in (src_ap, dst_ap, src_ap if upper is None else upper)]
                        lo = [a[0][:, :, 0, :], a[1][:, :, 0, :]]
                        hi = [a[2][:, :, 1, :], a[1][:, :, 1, :]]
                    else:
                        q = 0 if descending else 1
                        a = [t.rearrange("p (b side g two k) -> p b side g two k", side=2, two=2, k=k_,
                                         g=outer // (2 * k_))
                             for t in (src_ap, dst_ap, src_ap if upper is None else upper)]
                        lo = [a[0][:, :, q, :, 0, :], a[1][:, :, q, :, 0, :]]
                        hi = [a[2][:, :, q, :, 1, :], a[1][:, :, q, :, 1, :]]
                    least, most = (hi, lo) if descending else (lo, hi)
                    c(nc.vector.tensor_tensor(least[1], lo[0], hi[0], ALU.min))
                    c(nc.vector.tensor_tensor(most[1], lo[0], hi[0], ALU.max))
                    return c.n

                ready = [0, 0]
                for lev in range(1, IN_LANE):
                    start = max(ready)
                    ready = [start, start]
                    for e in reversed(range(lev)):
                        for d in range(2):
                            ready[d] = order(keys[at], keys[1 - at], 1 << e, 1 << lev, 1 - d, ready[d])
                        at = 1 - at
                dve.wait_ge(s_chain[k], max(ready))
                c(nc.vector.tensor_scalar(keys[1 - at], keys[at], signs[:, 0:1], None, ALU.mult))
                at = 1 - at
                ready = [c.n, c.n]
                for s in range(ACROSS + 1):
                    if s > 0:
                        for h in range(2):
                            dve.wait_ge(s_turn[k][h], s)
                            source, upper = psA[h][:, :], turned[s % 2][:, h, :]
                            view = "p (g two k) -> p g two k"
                            c(nc.vector.tensor_copy(upper.rearrange(view, two=2, k=TURNS << (s - 1))[:, :, 1, :],
                                                    source.rearrange(view, two=2, k=TURNS << (s - 1))[:, :, 1, :]))
                            after = c.n
                            for e in reversed(range(s)):
                                to = turned[e % 2][:, h, :]
                                if s < ACROSS:
                                    order(source, to, TURNS << e, TURNS << s, True, after, upper)
                                    after = order(source, to, TURNS << e, TURNS << s, False, 0, upper)
                                else:
                                    after = order(source, to, TURNS << e, 0, None, after, upper)
                                source, upper = to, None
                            dve.wait_ge(s_chain[k], c.n)
                            nc.vector.memset(mark[:], 0.0).then_inc(s_cross[k][h], 1)
                        for h in range(2):
                            dve.wait_ge(s_signed[k][h], s)
                        at = 0
                        ready = [c.n, c.n]
                    ready[0] = ready[1] = order(keys[at], keys[1 - at], HALF, 0, None, max(ready))
                    at = 1 - at
                    start_at = at
                    steps = [(e, h) for e in reversed(range(3, IN_LANE - 1)) for h in range(2)]
                    steps += [(e, h) for h in range(2) for e in reversed(range(3))]
                    for e, h in steps:
                        src_b = (start_at + (IN_LANE - 2 - e)) % 2
                        cut = slice(h * HALF, (h + 1) * HALF)
                        ready[h] = order(keys[src_b][:, cut], keys[1 - src_b][:, cut], 1 << e, 0, None, ready[h])
                        if e == 0:
                            assert src_b == 1
                            dve.wait_ge(s_chain[k], ready[h])
                            nc.vector.memset(mark[:], 0.0).then_inc(s_lane[k][h], 1)
                    at = 0

            def bucket_counts(k):
                dve.wait_ge(s_above, k + 1)
                v.link(nc.vector.memset(above[:], 0.0))
                v.link(nc.vector.memset(above[:, 0:1], float(P * NCOL)))
                v.link(nc.vector.tensor_scalar(above[:, 1:NS], (psE if k else psC[0])[:, 0:NB], 0.5, 0.5 * P * NCOL, ALU.mult, ALU.add))
                v.link(nc.vector.tensor_tensor(n_all[:], above[:, 0:NS], above[:, 1:NS + 1], ALU.subtract))
                v.link(nc.vector.tensor_scalar(n_tile_i[:], n_all[:], float(P - 1), None, ALU.add))
                v.link(nc.vector.tensor_scalar(n_tile_i[:], n_tile_i[:], LOW_BITS, None, ALU.arith_shift_right))
                v.link(nc.vector.tensor_copy(n_tile[:], n_tile_i[:]))
                v.link(nc.vector.scalar_tensor_tensor(out=excess[:], in0=n_tile[:], scalar=-float(P), in1=n_all[:],
                                                      op0=ALU.mult, op1=ALU.add))

            Hf, Xf = H[:, :, :], X[:, :, :]

            def wide(t):
                return t[:].rearrange("p (b a) -> p b a", a=1).to_broadcast([P, NS, D])

            def norm_stats(k):
                v.link(nc.vector.tensor_reduce(mean[:], Xf, AX.X, ALU.add))
                v.link(nc.vector.tensor_scalar(mean[:], mean[:], 1.0 / D, None, ALU.mult))
                v.link(nc.vector.tensor_tensor(Hf, Xf, wide(mean), ALU.subtract))
                v.link(nc.vector.tensor_tensor(T1[:, :, :], Hf, Hf, ALU.mult))
                v.link(nc.vector.tensor_reduce(var[:], T1[:, :, :], AX.X, ALU.add))
                nc.vector.tensor_scalar(var[:], var[:], 1.0 / D, EPS, ALU.mult, ALU.add).then_inc(s_var[k], 1)

            def norm_rest(k):
                dve.wait_ge(s_root[k], 1)
                v.link(nc.vector.reciprocal(rstd[:], rstd[:]))
                v.link(nc.vector.tensor_tensor(Hf, Hf, wide(rstd), ALU.mult))
                nc.vector.tensor_scalar(Hf, Hf, 0.0, None, ALU.max).then_inc(s_h[k], 1)
                dve.wait_ge(s_h[k], 1)

            dve.wait_ge(s_x, 32)
            norm_stats(0)
            dve.wait_ge(s_edges, 16 * 6)
            di = gotf[:, 0:LANE].bitcast(I32)
            dj = gotf[:, LANE:2 * LANE].bitcast(I32)
            v.link(nc.vector.tensor_scalar(di[:, 0:NCOL], dst_i[:], LOW_BITS, None, ALU.arith_shift_right))
            v.link(nc.vector.tensor_copy(bkt_b[:, 0:NCOL], di[:, 0:NCOL]))
            v.link(nc.vector.tensor_scalar(nxt_i, nxt_i, LOW_BITS, None, ALU.arith_shift_right))
            v.link(nc.vector.tensor_tensor(dj[:, 0:NCOL], di[:, 0:NCOL], nxt_i, ALU.is_gt))
            nc.vector.tensor_reduce(flag[:, 0:1], dj[:, 0:NCOL], AX.X, ALU.add).then_inc(s_flagd, 1)
            v.link(nc.vector.tensor_scalar(di[:, 0:NCOL], dst_i[:], P - 1, None, ALU.bitwise_and))
            v.link(nc.vector.tensor_copy(low_b[:, 0:NCOL], di[:, 0:NCOL]))
            nc.vector.tensor_copy(pair1[:, :, 0], dst_i[:])
            nc.vector.tensor_copy(pair1[:, :, 1], src_i[:]).then_inc(s_pair, 1)
            dve.wait_ge(s_flagp, 1)
            nc.vector.tensor_scalar(flag_i[:], psD[0:1, 0:1], 1.0, None, ALU.min).then_inc(s_flag, 1)
            norm_rest(0)

            dve.wait_ge(s_flag, 1)
            unsorted = dve.value_load(flag_i[0:1, 0:1], min_val=0, max_val=1)
            v0 = v
            with dve.If(unsorted > 0):
                v = Chain(dve, s_vf)
                pack(dst_i, src_i)
                sort(0)
                ki, kj = keys[0].bitcast(I32), keys[1].bitcast(I32)
                v.link(nc.vector.tensor_scalar(back_pair[:, :, 1], ki, (1 << PARTNER_BITS) - 1, None, ALU.bitwise_and))
                v.link(nc.vector.tensor_scalar(kj, ki, BUCKET_AT, 63, ALU.logical_shift_right, ALU.bitwise_and))
                v.link(nc.vector.tensor_scalar(kj, kj, LOW_BITS, None, ALU.logical_shift_left))
                v.link(nc.vector.tensor_scalar(ki, ki, PARTNER_BITS, P - 1, ALU.logical_shift_right, ALU.bitwise_and))
                nc.vector.tensor_tensor(back_pair[:, :, 0], ki, kj, ALU.bitwise_or).then_inc(s_pair, 1)
                dve.wait_ge(s_pair, 2)
            with dve.Else():
                dve.wait_ge(s_flag, 1)
            v = v0

            pack(src_i, dst_i)
            bucket_counts(0)
            v.link(nc.vector.tensor_scalar(need[:], excess[:, 0:NB], -1.0, None, ALU.mult))
            v.link(nc.vector.tensor_tensor(pad_on[:], need[:], lane_i[:], ALU.is_gt))
            v.link(nc.vector.copy_predicated(keys[0][:, NCOL:NCOL + NB], pad_on[:], pads_i[:].bitcast(F32)))
            sort(1)

            bucket_counts(1)
            nc.vector.tensor_tensor_scan(tile_end[:], ones[:, 0:NS], n_tile[:], 0.0, ALU.mult, ALU.add).then_inc(s_cols, 1)
            dve.wait_ge(s_packed, 2)
            nc.vector.tensor_scalar(partner[:, 0:NT], packed[:], (1 << PARTNER_BITS) - 1, None, ALU.bitwise_and)
            nc.vector.memset(partner[:, NT:NTP], 0)
            v.link(nc.vector.tensor_scalar(tile_b0[:, 0:NT], packed[0:1, :], BUCKET_AT, 63,
                                           ALU.logical_shift_right, ALU.bitwise_and))
            nc.vector.memset(tile_b0[:, NT:NTP], NB)
            v.link(nc.vector.tensor_scalar(packed[:], packed[:], PARTNER_BITS, 2 * P - 1,
                                           ALU.logical_shift_right, ALU.bitwise_and))
            v.link(nc.vector.tensor_copy(key_l[:, 0:NT], packed[:]))
            nc.vector.memset(key_l[:, NT:NTP], float(2 * P)).then_inc(s_edge0, 1)
            dve.wait_ge(s_colT, 1)
            v.link(nc.vector.tensor_copy(cols[:, 0:1], psE[0:NS, 128:129]))
            v.link(nc.vector.tensor_copy(cols[:, 1:2], psE[0:NS, 256:257]))
            nc.vector.tensor_scalar(begun[0:NS, :], iota_t[0:NS, :], cols[:, 0:1], None, ALU.is_ge).then_inc(s_begun, 1)
            dve.wait_ge(s_tile, 1)
            for m in range(2):
                half = slice(m * HT, (m + 1) * HT)
                nc.vector.tensor_scalar(base1[:, half], psC[m][:, 0:HT], float(P), None, ALU.mult)
                nc.vector.tensor_copy(tile_b1[:, half], psC[m][0:1, 0:HT])
                ins = nc.vector.scalar_tensor_tensor(
                    out=tile_s1[:, half], in0=iota_t[0:1, half], scalar=float(P),
                    in1=(psE if m else psD)[0:1, 0:HT], op0=ALU.mult, op1=ALU.add)
            ins.then_inc(s_tiled, 1)
            dve.wait_ge(s_tiled, 1)
            nc.vector.memset(sums[:, :, :], 0.0).then_inc(s_add[0], 1)

            def degree_hots(G0, i, g):
                for hot_out, n, key in ((low_hot, P, low_b), (bkt_hot, NS, bkt_b)):
                    ins = nc.vector.tensor_tensor(
                        hot_out[:], iota_b[:, 0:n].rearrange("p (a n) -> p a n", a=1).to_broadcast([P, GRP, n]),
                        key[:, bass.ds(i * TPI + g * GRP, GRP)].rearrange("p (c a) -> p c a", a=1).to_broadcast([P, GRP, n]),
                        ALU.is_equal)
                ins.then_inc(s_hots, 1)

            def keep_rows(base):
                dve.wait_ge(s_rows, 32)
                for g in range(GROUPS + 1):
                    T = P if g < GROUPS - 1 else TAIL
                    if g < GROUPS:
                        if g >= 1:
                            dve.wait_ge(s_rowT, g)
                        nc.vector.tensor_copy(rows_f[0:T, :], rows[0:T, g, :]).then_inc(s_rowf, 1)
                    if g >= 1:
                        T = P if g - 1 < GROUPS - 1 else TAIL
                        dve.wait_ge(s_rowT, g)
                        c = slice((g - 1) * P, (g - 1) * P + T)
                        nc.vector.tensor_tensor(key_l[:, c], psA[(g - 1) % 2][:, 0:T], base[:, c], ALU.subtract)
                        nc.vector.tensor_copy(partner[:, c], psA[(g - 1) % 2][:, P:P + T]).then_inc(s_rowk, 1)
                dve.wait_ge(s_rowk, GROUPS)

            def one_hots(k, g, i, off):
                for j in range(GRP):
                    ins = nc.vector.tensor_scalar(hot[:, g, j, :], iota_n[:], key_l[:, bass.ds(i * TPI + (off * GRP + j), 1)],
                                                  None, ALU.is_equal)
                ins.then_inc(s_hot[k], 1)

            def add_parts(k, tile_b, width, p, i, off, after):
                dve.wait_ge(s_part[k], after + 1)
                for j in range(GRP):
                    b = dve.value_load(tile_b[0:1, bass.ds(i * TPI + (off * GRP + j), 1)], min_val=0, max_val=NB)
                    at = sums[:, bass.ds(b, 1), 0:width].rearrange("p a d -> p (a d)")
                    dve.wait_ge(s_add[k], after * GRP + (j + 1))
                    ins = nc.vector.tensor_tensor(at, at, psC[p][:, j * width:(j + 1) * width], ALU.add)
                    ins.then_inc(s_add[k], 1)

            def attention(i, first):
                for g in range(GPI):
                    p = g % 2
                    G0 = i * GPI + g
                    dve.wait_ge(s_q, G0 + 1)
                    dve.wait_ge(s_got[0][g], i * 64 + 64)
                    rows4 = got[:, g * GRP:(g + 1) * GRP, :]
                    nc.vector.tensor_tensor(prod[:], psB[p][:, 0:GRP * D].rearrange("p (t d) -> p t d", d=D),
                                            rows4[:, :, 0:D], ALU.mult).then_inc(s_prod, 1)
                    dve.wait_ge(s_prod, G0 + 1)
                    if not (first and g < 2):
                        dve.wait_ge(s_exp, G0 - 1)
                    nc.vector.tensor_reduce(score[:, p, :], prod[:].rearrange("p t (h d) -> p (t h) d", d=DH),
                                            AX.X, ALU.add).then_inc(s_red, 1)
                    dve.wait_ge(s_red, G0 + 1)
                    nc.vector.tensor_scalar(score[:, p, :], score[:, p, :], -CLIP, CLIP, ALU.max, ALU.min
                                            ).then_inc(s_score, 1)
                    if not (first and g < 2):
                        dve.wait_ge(s_part[0], G0 - 1)
                    one_hots(0, (g + 2) % 4, i, g + 2)
                    if not (first and g == 0):
                        dve.wait_ge(s_degmm, G0)
                    degree_hots(G0, i, g)
                    dve.wait_ge(s_exp, G0 + 1)
                    nc.vector.tensor_tensor(
                        msg[:, p, :, 0:D].rearrange("p t (h d) -> p t h d", h=HEADS),
                        rows4[:, :, D:2 * D].rearrange("p t (h d) -> p t h d", h=HEADS),
                        msg[:, p, :, D:MSG].rearrange("p t (h a) -> p t h a", a=1).to_broadcast([P, GRP, HEADS, DH]),
                        ALU.mult).then_inc(s_msg, 1)
                    if not (first and g == 0):
                        add_parts(0, tile_b0, MSG, 1 - p, i, g - 1, G0 - 1)

            one_hots(0, 0, 0, 0)
            one_hots(0, 1, 0, 1)
            attention(0, True)
            with dve.Fori(1, ITERS) as i:
                attention(i, False)
            last = NT // GRP - 1
            add_parts(0, tile_b0, MSG, last % 2, ITERS - 1, GPI - 1, last)

            dve.wait_ge(s_add[0], NT + 1)
            weights = sums[:, :, D:MSG]
            v.link(nc.vector.tensor_scalar(weights, weights, 1e-8, None, ALU.add))
            v.link(nc.vector.reciprocal(weights, weights))
            v.link(nc.vector.tensor_tensor(
                T1[:, :, :].rearrange("p b (h d) -> p b h d", h=HEADS),
                sums[:, :, 0:D].rearrange("p b (h d) -> p b h d", h=HEADS),
                weights.rearrange("p b (h a) -> p b h a", a=1).to_broadcast([P, NS, HEADS, DH]), ALU.mult))
            v.link(nc.vector.tensor_tensor(T1[:, :, :], T1[:, :, :], Hf, ALU.add))
            v.link(nc.vector.tensor_tensor(Xf, Xf, T1[:, :, :], ALU.add))
            dve.wait_ge(s_degmm, NT // GRP)
            nc.vector.tensor_scalar(deg[:], psD[:, 0:NS], 1.0, None, ALU.add).then_inc(s_degr, 1)
            norm_stats(1)
            dve.wait_ge(s_degroot, 1)
            nc.vector.reciprocal(dinv[:], root[:]).then_inc(s_dinv, 1)
            norm_rest(1)
            nc.vector.memset(sums[:, :, :], 0.0).then_inc(s_add[1], 1)
            keep_rows(base1)

            def convolve(i, first):
                for g in range(GPI):
                    p = g % 2
                    G0 = i * GPI + g
                    if not first:
                        dve.wait_ge(s_part[1], G0 - (GPI - 1))
                    one_hots(1, g, i, g)
                    if not (first and g == 0):
                        add_parts(1, tile_b1, D, 1 - p, i, g - 1, G0 - 1)

            convolve(0, True)
            with dve.Fori(1, ITERS) as i:
                convolve(i, False)
            add_parts(1, tile_b1, D, last % 2, ITERS - 1, GPI - 1, last)

            dve.wait_ge(s_add[1], NT + 1)
            dve.wait_ge(s_g, NS)
            dve.wait_ge(s_pq[1], NS)
            T = T1[:, :, :]
            v.link(nc.vector.tensor_tensor(T, sums[:, :, 0:D], G[:, :, :], ALU.add))
            v.link(nc.vector.tensor_tensor(T, T, wide(dinv), ALU.mult))
            v.link(nc.vector.tensor_tensor(T, T, Q[:, :, :], ALU.add))
            for n in range(2):
                v.link(nc.vector.tensor_tensor(T, T, bias2[:, n:n + 1, :].to_broadcast([P, NS, D]), ALU.add))
            nc.vector.tensor_scalar(G[:, :, :], T, 20.0, None, ALU.min).then_inc(s_y, 1)
            dve.wait_ge(s_ye, 1)
            v.link(nc.vector.scalar_tensor_tensor(out=Hf, in0=Hf, scalar=2.0, in1=Hf, op0=ALU.add, op1=ALU.mult))
            v.link(nc.vector.tensor_scalar(G[:, :, :], Hf, 2.0, None, ALU.add))
            v.link(nc.vector.reciprocal(G[:, :, :], G[:, :, :]))
            v.link(nc.vector.tensor_tensor(Hf, Hf, G[:, :, :], ALU.mult))
            v.link(nc.vector.tensor_tensor(T, T, Hf, ALU.mult))
            nc.vector.tensor_tensor(T, T, Xf, ALU.add).then_inc(s_fin, 1)


_INS = ["x", "src", "dst", "L0_gnn_qW", "L0_gnn_kW", "L0_gnn_vW", "L1_gnn_W_gcn", "L1_gnn_b_gcn",
        "L1_gnn_W_lin", "L1_gnn_b_lin"]


def kernel(**inputs):
    import numpy as _np
    import concourse.bacc as _bacc
    from concourse import mybir as _mybir
    from concourse.bass_utils import run_bass_kernel_spmd as _run

    nc = _bacc.Bacc("TRN2", target_bir_lowering=False, num_devices=1)
    arrays, args = {}, []
    for name in _INS:
        a = _np.ascontiguousarray(inputs[name])
        arrays[f"in_{name}"] = a
        args.append(nc.dram_tensor(f"in_{name}", a.shape, _mybir.dt.from_np(a.dtype), kind="ExternalInput").ap())
    args.append(nc.dram_tensor("out_x", inputs["x"].shape, _mybir.dt.float32, kind="ExternalOutput").ap())
    gnn_kernel(nc, *args)
    r = _run(nc, [arrays], core_ids=[0])
    return r.results[0]["out_x"]
```

```python
from contextlib import ExitStack

import concourse.bass as bass
from concourse import mybir

ALU = mybir.AluOpType
ACT = mybir.ActivationFunctionType
AX = mybir.AxisListType
F32 = mybir.dt.float32
BF16 = mybir.dt.bfloat16
I32 = mybir.dt.int32

P = 128
HEADS = 4
EPS = 1e-5
CLIP = 10.0
GRP = 4
GPI = 4
LEAD = 2 * GRP
TPI = GRP * GPI
NODE_BITS, NORMAL_BIT = 13, 27
LOW_BITS = 7
ANY_NODE = (1 << NODE_BITS) - 1


class Chain:

    def __init__(self, eng, sem):
        self.eng, self.sem, self.n = eng, sem, 0

    def __call__(self, ins):
        ins.then_inc(self.sem, 1)
        self.n += 1

    def wait(self, but=0):
        if self.n > but:
            self.eng.wait_ge(self.sem, self.n - but)

    def link(self, ins):
        self(ins)
        self.wait()


def gnn_kernel(nc, x, src, dst, qW, kW, vW, W_gcn, b_gcn, W_lin, b_lin, out):
    N, D = x.shape
    E = src.shape[0]
    DH = D // HEADS
    MSG = D + HEADS
    NB = -(-N // P)
    NS = NB + 1
    FULL = N // P
    REST = N - FULL * P
    NCOL = -(-E // (P * TPI)) * TPI
    LAST = E - (P - 1) * NCOL
    PAD_KEY = NB * P
    NT = -(-((E + NB * (P - 1)) // P) // TPI) * TPI
    NTP = NT + TPI
    GROUPS = NT // P + 1
    TAIL = NT - (GROUPS - 1) * P
    HT = NTP // 2
    ITERS = NT // TPI
    LANE = 1024
    HALF = LANE // 2
    IN_LANE = LANE.bit_length() - 1
    ALONE = 5
    ACROSS = P.bit_length() - 1
    TURNS = HALF // P
    NEVER = (1 << NORMAL_BIT) | (ANY_NODE << NODE_BITS)
    SIDE = 64
    FIRST_ROWS = 4
    assert 0 < LAST <= NCOL and HT + GROUPS <= 512 and 0 < TAIL < P and NCOL <= NT
    assert NCOL <= LANE and NS * P <= ANY_NODE and NS < SIDE and -(-E // P) + NB - 1 <= NT
    assert GROUPS * P <= NTP and P * NCOL % LANE == 0 and FIRST_ROWS < GROUPS <= 2 * FIRST_ROWS
    PER = NS // 5
    UNIT = PER // 2
    CHUNKS = [(b, b + PER) for b in range(0, NS, PER)]
    assert NS == 5 * PER and PER == 2 * UNIT
    BACK = P * NCOL // LANE

    ctx = ExitStack()
    with ctx:
        def sb(name, shape, dt=F32):
            return ctx.enter_context(nc.sbuf_tensor(name, shape, dt))

        def ps(name):
            return ctx.enter_context(nc.psum_tensor(name, [P, 512], F32))

        def sem(name):
            return ctx.enter_context(nc.semaphore(name))

        kv_table = nc.dram_tensor("kv_table", [NS * P, 2 * D], F32, kind="Internal").ap()
        g_table = nc.dram_tensor("g_table", [NS * P, D], F32, kind="Internal").ap()
        list0 = nc.dram_tensor("list0", [P * NCOL], I32, kind="Internal").ap()
        list1 = nc.dram_tensor("list1", [P * NCOL, 2], I32, kind="Internal").ap()

        X = sb("X", [P, NS, D])
        H = sb("H", [P, NS, D])
        Q = sb("Q", [P, NS, D])
        T1 = sb("T1", [P, NS, D])
        sums = sb("sums", [P, NS, MSG])
        G = sb("G", [P, NS, D])
        gf = G[:, :, :].rearrange("p b d -> p (b d)")
        back_pair = gf[:, 0:2 * LANE].bitcast(I32).rearrange("p (c k) -> p c k", k=2)
        nxt_i = gf[:, 2 * LANE:2 * LANE + NCOL].bitcast(I32)
        sign_out = gf[:, 2 * LANE + NCOL:2 * LANE + 2 * NCOL].bitcast(BF16).rearrange("p (k c) -> p k c", k=2)

        src_i = sb("src_i", [P, NCOL], I32)
        dst_i = sb("dst_i", [P, NCOL], I32)
        bkt_b = sb("bkt_b", [P, NT], BF16)
        low_b = sb("low_b", [P, NT], BF16)
        pair1 = sb("pair1", [P, NCOL, 2], I32)

        t1f = T1[:, :, :].rearrange("p b d -> p (b d)")
        keys = [t1f[:, n * LANE:(n + 1) * LANE] for n in range(2)]
        plain = t1f[:, 2 * LANE:3 * LANE]
        lane_i = sb("lane_i", [P, 1], I32)
        signs = sb("signs", [P, ACROSS + 1])
        sign_i = sb("sign_i", [P, ACROSS + 1], I32)
        bounds = sb("bounds", [P, NB])
        over = sb("over", [P, 2, NB])

        rows = sb("rows", [P, GROUPS, 2 * P], I32)
        rows_f = sb("rows_f", [P, 2 * P])
        key_l = sb("key_l", [P, NTP])
        partner = sb("partner", [P, NTP], I32)
        base1 = sb("base1", [P, NTP])
        node_i = sb("node_i", [P, NT], I32)
        tile_b0 = sb("tile_b0", [1, LEAD + NTP], I32)
        tile_b1 = sb("tile_b1", [1, LEAD + NTP], I32)
        tile_iota = sb("tile_iota", [P, GROUPS])
        tile_row = sb("tile_row", [P, 2, GROUPS])
        tile_row_i = sb("tile_row_i", [P, 2, GROUPS], I32)
        sums_flat = sums[:, :, :].rearrange("p b m -> p (b m)")
        iota_t = sums_flat[:, 0:NTP]
        begun = sums_flat[:, NTP:2 * NTP]

        iota_n = sb("iota_n", [P, P])
        iota_b = sb("iota_b", [P, P], BF16)
        diff = sb("diff", [P, P])
        ident = sb("ident", [P, P])
        ident_b = sb("ident_b", [P, P], BF16)
        ones = sb("ones", [P, P])
        zero_b = sb("zero_b", [P, P], BF16)
        qkv_w = sb("qkv_w", [D, 3 * D])
        gl_w = sb("gl_w", [D, 2 * D])
        bias2 = sb("bias2", [P, 2, D])

        above = sb("above", [P, 2, NS + 1])
        n_all = sb("n_all", [P, 2, NS])
        n_tile = sb("n_tile", [P, 2, NS])
        first_row = sb("first_row", [P, 2, NS + 1])
        next_row = sb("next_row", [P, 2, NS + 1])
        start_i = sb("start_i", [P, 2, NS + 1], I32)
        tile_end = sb("tile_end", [P, 2, SIDE])
        shift = sb("shift", [P, 2, SIDE])
        cols = sb("cols", [P, 2])
        flag = sb("flag", [P, 2])
        flag_i = sb("flag_i", [1, 1], I32)
        mean = sb("mean", [P, NS])
        var = sb("var", [P, NS])
        rstd = sb("rstd", [P, NS])
        deg = sb("deg", [P, NS])
        root = sb("root", [P, NS])
        dinv = sb("dinv", [P, NS])

        stage = sb("stage", [P, 2, UNIT, D])
        hT = sb("hT", [D, 2, P])
        got = sb("got", [P, TPI, 2 * D])
        low_hot = sb("low_hot", [P, GRP, P], BF16)
        bkt_hot = sb("bkt_hot", [P, GRP, NS], BF16)
        gotf = got[:, :, :].rearrange("p t w -> p (t w)")
        turned = [gotf[:, n * LANE:(n + 1) * LANE].rearrange("p (h c) -> p h c", h=2) for n in range(2)]
        idx_ring = sb("idx_ring", [P, TPI], I32)
        hot = sb("hot", [P, 4, GRP, P])
        hot_b = sb("hot_b", [P, 4, GRP, P], BF16)
        kv_stage = hot[:, :, :, :].rearrange("p a t n -> p (a t n)")[:, 0:PER * 2 * D].rearrange(
            "p (b w) -> p b w", w=2 * D)
        hotT = sb("hotT", [P, 2, GRP * P])
        src_f, dst_f = src_i[:].bitcast(F32), dst_i[:].bitcast(F32)
        prod = src_f[:, 0:GRP * D].rearrange("p (t d) -> p t d", d=D)
        score = src_f[:, GRP * D:GRP * D + 2 * GRP * HEADS].rearrange("p (n c) -> p n c", n=2)
        msg = dst_f[:, 0:2 * GRP * MSG].rearrange("p (n t m) -> p n t m", n=2, t=GRP)

        psA = [ps("psA0"), ps("psA1")]
        psB = [ps("psB0"), ps("psB1")]
        turned_hot = [psA[n][:, 0:GRP * P // 2].bitcast(BF16) for n in range(2)]
        psC = [ps("psC0"), ps("psC1")]
        psD = ps("psD")
        psE = ps("psE")
        bucket_ps = [psC, [psD, psE]]

        s_edges = sem("edges_loaded")
        s_x = sem("x_loaded")
        s_w = sem("weights_loaded")
        s_pads = sem("pads_set")
        s_iota = sem("iota_made")
        s_const = sem("constants_made")
        s_a = sem("counts_made")
        s_rowidx = sem("tile_rows_made")
        s_list0 = sem("list0_written")
        s_rows0 = [sem("rows0_loaded_a"), sem("rows0_loaded_b")]
        s_turned0 = sem("rows0_turned")
        s_chain_rows = sem("tile_rows_float")
        s_pln = sem("layer_norm0_chain")
        s_above = sem("counts_on_pe")
        s_cols = sem("rows_for_columns")
        s_colT = sem("columns_turned")
        s_begun = sem("begun_made")
        s_tile = sem("tile_data_on_pe")
        s_tiled = sem("tile_data_kept")
        s_vf = sem("vector_chain_unsorted")
        s_stat = sem("inverse_roots0")
        s_scaled = sem("activations_scaled0")
        s_act = [sem("activations0"), sem("activations1")]
        s_xh = sem("residual0_added")
        s_mish = sem("mish_factors_made")
        s_v = sem("vector_chain")
        s_flagp = sem("disorder_counted")
        s_flagd = sem("disorder_marked")
        s_flag = sem("flag_made")
        s_chain = [sem("sort_chain1"), sem("sort_chain0")]
        s_lane = [[sem(f"lane_done{k}{h}") for h in range(2)] for k in range(2)]
        s_plain = [[sem(f"signs_off{k}{h}") for h in range(2)] for k in range(2)]
        s_turn = [[sem(f"sort_turned{k}{h}") for h in range(2)] for k in range(2)]
        s_cross = [[sem(f"cross_done{k}{h}") for h in range(2)] for k in range(2)]
        s_back = [[sem(f"sort_back{k}{h}") for h in range(2)] for k in range(2)]
        s_signed = [[sem(f"signs_on{k}{h}") for h in range(2)] for k in range(2)]
        s_pair = sem("pairs_made")
        s_list1 = sem("list1_written")
        s_var = [sem("variance0"), sem("variance1")]
        s_root = [sem("root0"), sem("root1")]
        s_degr = sem("degree_plus_one")
        s_degroot = sem("degree_root")
        s_dinv = sem("degree_inverse_root")
        s_pstage = [sem("p_staged0"), sem("p_staged1")]
        s_pT = [sem("p_turned0"), sem("p_turned1")]
        s_phT = [sem("p_kept0"), sem("p_kept1")]
        s_pmm = [sem("p_product0"), sem("p_product1")]
        s_pkv = [sem("table_rows_made0"), sem("table_rows_made1")]
        s_sstage = sem("skip_staged")
        s_sT = sem("skip_turned")
        s_shT = sem("skip_turned_kept")
        s_smm = sem("skip_product")
        s_tab = [[sem("table0_a"), sem("table0_b")], [sem("table1_a"), sem("table1_b")]]
        s_hots = sem("degree_hots")
        s_degmm = sem("degree_products")
        s_rows = sem("rows_loaded")
        s_rowf = sem("rows_float")
        s_rowT = sem("rows_turned")
        s_rowk = sem("rows_kept")
        s_edge0 = sem("edges0_unpacked")
        s_add = [sem("tiles_added0"), sem("tiles_added1")]
        s_idx = [sem("indices0"), sem("indices1")]
        s_got = [[sem(f"gathered{k}_{g}") for g in range(GPI)] for k in range(2)]
        s_hot = [sem("hot0"), sem("hot1")]
        s_wide = sem("hot_widened")
        s_hotp = sem("hot_turned")
        s_hotT = sem("hot_turned_kept")
        s_q = sem("queries_of_edges")
        s_prod = sem("query_key_products")
        s_red = sem("scores_summed")
        s_score = sem("scores_clipped")
        s_exp = sem("exponentials")
        s_msg = sem("messages_made")
        s_part = [sem("bucket_parts0"), sem("bucket_parts1")]
        s_y = sem("final_exp_in")
        s_ye = sem("final_exp_out")
        s_esq = sem("final_squares")
        s_den = sem("denominators")
        s_skip = sem("skip_and_self_loop")
        s_addend = sem("addends_made")
        s_fin = sem("result_made")
        s_out = sem("result_stored")
        s_pool = sem("pool_waited")

        def per_p(flat, n=NCOL):
            return flat.rearrange("(p c) -> p c", c=n)

        def wide(t, b0, b1):
            return t[:, b0:b1].rearrange("p (b a) -> p b a", a=1).to_broadcast([P, b1 - b0, D])

        block = ctx.enter_context(nc.Block())

        @block.sync
        def _(sp):
            sp.wait_ge(s_pads, 1)
            body = (P - 1) * NCOL
            sp.dma_start(src_i[0:P - 1, :], per_p(src[0:body])).then_inc(s_edges, 16)
            sp.dma_start(src_i[P - 1:P, 0:LAST], src[body:E].rearrange("(p c) -> p c", p=1)).then_inc(s_edges, 16)
            sp.dma_start(dst_i[0:P - 1, :], per_p(dst[0:body])).then_inc(s_edges, 16)
            sp.dma_start(dst_i[P - 1:P, 0:LAST], dst[body:E].rearrange("(p c) -> p c", p=1)).then_inc(s_edges, 16)
            sp.dma_start(nxt_i[0:P - 1, :], per_p(dst[1:body + 1])).then_inc(s_edges, 16)
            sp.dma_start(nxt_i[P - 1:P, 0:LAST - 1], dst[body + 1:E].rearrange("(p c) -> p c", p=1)).then_inc(s_edges, 16)
            sp.dma_start(X[:, 0:FULL, :], x[0:FULL * P, :].rearrange("(b p) d -> p b d", p=P)).then_inc(s_x, 16)
            sp.dma_start(X[0:REST, FULL, :], x[FULL * P:N, :]).then_inc(s_x, 16)
            def store_table(k, table):
                blocks = table.rearrange("(b p) w -> p b w", p=P)
                with sp.Fori(0, NS // PER) as i:
                    for u in range(2):
                        sp.wait_ge(s_pkv[k], i * PER + (u + 1) * UNIT)
                        at = i * PER + u * UNIT
                        sp.dma_start(blocks[:, bass.ds(at, UNIT), :],
                                     G[:, bass.ds(at, UNIT), :] if k else
                                     kv_stage[:, u * UNIT:(u + 1) * UNIT, :]).then_inc(s_tab[k][u], 16)

            store_table(0, kv_table)
            for h in range(2):
                sp.wait_ge(s_lane[1][h], ACROSS + 1)
                cut = slice(h * HALF, (h + 1) * HALF)
                sp.dma_start(list0.rearrange("(p c) -> p c", c=LANE)[:, cut],
                             keys[0][0:BACK, cut].bitcast(I32)).then_inc(s_list0, 16)

            store_table(1, g_table)

            for n, (b0, b1) in enumerate(CHUNKS):
                sp.wait_ge(s_fin, n + 1)
                full = min(b1, FULL)
                sp.dma_start(out[b0 * P:full * P, :].rearrange("(b p) d -> p b d", p=P), T1[:, b0:full, :]).then_inc(s_out, 16)
            sp.dma_start(out[FULL * P:N, :], T1[0:REST, FULL, :]).then_inc(s_out, 16)
            sp.wait_ge(s_out, 16 * (len(CHUNKS) + 1))

        @block.gpsimd
        def _(pool):
            nc.gpsimd.iota(iota_t, [[1, NTP]], base=0, channel_multiplier=0,
                           allow_small_or_imprecise_dtypes=True).then_inc(s_iota, 1)
            nc.gpsimd.iota(iota_n[:], [[1, P]], base=0, channel_multiplier=0,
                           allow_small_or_imprecise_dtypes=True).then_inc(s_iota, 1)
            nc.gpsimd.iota(diff[:], [[1, P]], base=0, channel_multiplier=-1,
                           allow_small_or_imprecise_dtypes=True).then_inc(s_iota, 1)
            nc.gpsimd.iota(tile_iota[:], [[P, GROUPS]], base=0, channel_multiplier=1,
                           allow_small_or_imprecise_dtypes=True).then_inc(s_iota, 1)
            nc.gpsimd.iota(lane_i[:], [[0, 1]], base=0, channel_multiplier=1).then_inc(s_iota, 1)

            def gather_list(k):
                pool.wait_ge(s_rowidx, 1)
                for g in range(GROUPS):
                    T = P if g < GROUPS - 1 else TAIL
                    nc.gpsimd.indirect_dma_start(
                        out=rows[0:T, g, :] if k else rows[0:T, g, 0:P], out_offset=None,
                        in_=list1.rearrange("(r l) k -> r (l k)", l=P) if k else list0.rearrange("(r l) -> r l", l=P),
                        in_offset=bass.IndirectOffsetOnAxis(ap=tile_row_i[0:T, k, g:g + 1], axis=0)
                    ).then_inc(s_rows if k else s_rows0[g // FIRST_ROWS], 16)

            def gather_list1():
                pool.wait_ge(s_list1, 16)
                gather_list(1)

            def gathers(k, table, width, free, after_first=None):
                def one(i, first):
                    for g in range(GPI):
                        pool.wait_ge(s_idx[k], i * GPI + (g + 1))
                        if not first:
                            pool.wait_ge(free, i * GPI + (g + 1 - GPI))
                        pool.sem_inc(s_pool, 1)
                        for j in range(GRP):
                            n = g * GRP + j
                            nc.gpsimd.indirect_dma_start(
                                out=got[:, n, 0:width], out_offset=None, in_=table,
                                in_offset=bass.IndirectOffsetOnAxis(ap=idx_ring[:, n:n + 1], axis=0)).then_inc(s_got[k][g], 16)
                one(0, True)
                if after_first:
                    after_first()
                with pool.Fori(1, ITERS) as i:
                    one(i, False)

            def stage_tiles(k):
                def one(i, first):
                    for u in range(2):
                        if k:
                            pool.wait_ge(s_act[k], i + 1)
                            pool.sem_inc(s_pool, 1)
                        if not first:
                            pool.wait_ge(s_pT[k], i * PER + ((u + 1) * UNIT - PER))
                            pool.sem_inc(s_pool, 1)
                        nc.gpsimd.tensor_copy(stage[:, u, :, :].rearrange("p b d -> p (b d)"),
                                              H[:, bass.ds(i * PER + u * UNIT, UNIT), :].rearrange("p b d -> p (b d)")
                                              ).then_inc(s_pstage[k], 1)
                one(0, True)
                with pool.Fori(1, NS // PER) as i:
                    one(i, False)

            pool.wait_ge(s_x, 32)
            chain = Chain(pool, s_pln)

            def row_sums(total, values):
                n, at = D // 2, values
                while n > 3:
                    chain.link(nc.gpsimd.tensor_tensor(Q[:, :, 0:n], at[:, :, 0:n], at[:, :, n:2 * n], ALU.add))
                    n, at = n // 2, Q
                chain.link(nc.gpsimd.tensor_tensor(Q[:, :, 0:3], Q[:, :, 0:3], Q[:, :, 3:6], ALU.add))
                column = total[:].rearrange("p (b a) -> p b a", a=1)
                chain.link(nc.gpsimd.tensor_tensor(column, Q[:, :, 0:1], Q[:, :, 1:2], ALU.add))
                chain.link(nc.gpsimd.tensor_tensor(column, column, Q[:, :, 2:3], ALU.add))

            assert D == 96
            row_sums(mean, X)
            chain.link(nc.gpsimd.tensor_scalar(mean[:], mean[:], 1.0 / D, None, ALU.mult))
            chain.link(nc.gpsimd.tensor_tensor(H[:, :, :], X[:, :, :], wide(mean, 0, NS), ALU.subtract))
            chain.link(nc.gpsimd.tensor_tensor(Q[:, :, :], H[:, :, :], H[:, :, :], ALU.mult))
            row_sums(var, Q)
            nc.gpsimd.tensor_scalar(var[:], var[:], 1.0 / D, EPS, ALU.mult, ALU.add).then_inc(s_var[0], 1)
            pool.wait_ge(s_stat, 1)
            nc.gpsimd.tensor_tensor(H[:, :, :], H[:, :, :], wide(rstd, 0, NS), ALU.mult).then_inc(s_scaled, 1)
            pool.wait_ge(s_scaled, 1)
            nc.gpsimd.tensor_scalar(H[:, :, :], H[:, :, :], 0.0, None, ALU.max).then_inc(s_act[0], 1)
            pool.wait_ge(s_act[0], 1)
            stage_tiles(0)
            nc.gpsimd.tensor_tensor(X[:, :, :], X[:, :, :], H[:, :, :], ALU.add).then_inc(s_xh, 1)
            pool.wait_ge(s_list0, 32)
            gather_list(0)
            for h in range(2):
                pool.wait_ge(s_tab[0][h], 16 * (NS // PER))
            gathers(0, kv_table, 2 * D, s_msg, gather_list1)
            stage_tiles(1)
            for h in range(2):
                pool.wait_ge(s_tab[1][h], 16 * (NS // PER))
            gathers(1, g_table, D, s_part[1])
            for n, (b0, b1) in enumerate(CHUNKS):
                pool.wait_ge(s_mish, n + 1)
                y, e = T1[:, b0:b1, :], H[:, b0:b1, :]
                chain.link(nc.gpsimd.tensor_tensor(e, e, G[:, b0:b1, :], ALU.mult))
                chain.link(nc.gpsimd.tensor_tensor(y, y, e, ALU.mult))
                nc.gpsimd.tensor_tensor(y, y, X[:, b0:b1, :], ALU.add).then_inc(s_fin, 1)

        @block.scalar
        def _(act):
            a = Chain(act, s_a)

            act.wait_ge(s_pads, 1)
            for n, w in enumerate((qW, kW, vW)):
                act.dma_start(qkv_w[:, n * D:(n + 1) * D], w).then_inc(s_w, 16)
            for n, w in enumerate((W_gcn, W_lin)):
                act.dma_start(gl_w[:, n * D:(n + 1) * D], w).then_inc(s_w, 16)
            for n, b in enumerate((b_gcn, b_lin)):
                act.dma_start(bias2[:, n, :], b.rearrange("(a d) -> a d", a=1).to_broadcast([P, D])).then_inc(s_w, 16)

            def root_of(k, n):
                cut = bass.ds(n * PER, PER) if k else slice(0, NS)
                act.wait_ge(s_var[k], n + 1)
                nc.scalar.activation(rstd[:, cut], var[:, cut], ACT.Sqrt).then_inc(s_root[k], 1)

            def count_above(k, key_i, buckets):
                for b in buckets:
                    a.wait(1)
                    a(nc.scalar.activation(sign_out[:, a.n % 2, :], key_i[:], ACT.Sign, bias=bounds[:, b:b + 1],
                                           accum_out=over[:, k, b:b + 1]))

            def sort_turns(k, between):
                for s in range(ACROSS):
                    for h in range(2):
                        cut = slice(h * HALF, (h + 1) * HALF)
                        act.wait_ge(s_lane[k][h], s + 1)
                        nc.scalar.activation(plain[:, cut], keys[0][:, cut], ACT.Copy,
                                             scale=signs[:, s:s + 1]).then_inc(s_plain[k][h], 1)
                    for h in range(2):
                        cut = slice(h * HALF, (h + 1) * HALF)
                        act.wait_ge(s_back[k][h], s + 1)
                        nc.scalar.activation(keys[0][:, cut], psB[h][:, :], ACT.Copy,
                                             scale=signs[:, s + 1:s + 2]).then_inc(s_signed[k][h], 1)
                    between(s)

            def projection(k):
                def keep_turned(b, j, first):
                    act.wait_ge(s_pT[k], b + 1)
                    if not (first and j < 2):
                        act.wait_ge(s_pmm[k], b - 1)
                    nc.scalar.copy(hT[:, j % 2, :], psA[j % 2][0:D, 0:P]).then_inc(s_phT[k], 1)

                def products(b, j, i, first):
                    bank = psB[j % 2]
                    act.wait_ge(s_pmm[k], b + 1)
                    if k == 0:
                        nc.scalar.copy(Q[:, bass.ds(b, 1), :].rearrange("p a d -> p (a d)"), bank[:, 0:D])
                        if j % UNIT == 0 and not first:
                            act.wait_ge(s_tab[k][j // UNIT], i * 16)
                        nc.scalar.copy(kv_stage[:, j, :], bank[:, D:3 * D]).then_inc(s_pkv[k], 1)
                    else:
                        nc.scalar.activation(G[:, bass.ds(b, 1), :].rearrange("p a d -> p (a d)"), bank[:, 0:D], ACT.Copy,
                                             scale=dinv[:, bass.ds(b, 1)]).then_inc(s_pkv[k], 1)

                def chunk(i, first=False, last=False):
                    keep_turned(i * PER, 0, first)
                    for j in range(PER):
                        if j + 1 < PER:
                            keep_turned(i * PER + (j + 1), j + 1, first)
                        products(i * PER + j, j, i, first)
                        if k and j == UNIT and not last:
                            root_of(1, i + 1)

                return chunk

            def feed(k, i, g):
                nc.scalar.copy(idx_ring[:, g * GRP:(g + 1) * GRP],
                               partner[:, bass.ds(i * TPI + g * GRP, GRP)]).then_inc(s_idx[k], 1)

            act.wait_ge(s_const, 1)
            act.wait_ge(s_edges, 16 * 6)
            count_above(0, src_i, range(NB))
            early = 3 * NB // 4
            count_above(1, dst_i, range(NB // 6))
            root_of(0, 0)
            count_above(1, dst_i, range(NB // 6, early))

            act.wait_ge(s_flag, 1)
            unsorted = act.value_load(flag_i[0:1, 0:1], min_val=0, max_val=1)
            with act.If(unsorted > 0):
                sort_turns(0, lambda s: None)
                act.wait_ge(s_pair, 2)
                act.dma_start(list1[0:BACK * LANE, :].rearrange("(p c) k -> p (c k)", p=BACK),
                              back_pair[0:BACK, :, :].rearrange("p c k -> p (c k)")).then_inc(s_list1, 16)
            with act.Else():
                act.wait_ge(s_pair, 1)
                act.dma_start(list1[0:P * NCOL, :].rearrange("(p c) k -> p (c k)", p=P),
                              pair1[:, :, :].rearrange("p c k -> p (c k)")).then_inc(s_list1, 16)

            project_chunk = projection(0)

            def between(s):
                if s < len(CHUNKS):
                    project_chunk(s, s == 0)
                    count_above(1, dst_i, range(early + s * (NB - early) // len(CHUNKS),
                                                early + (s + 1) * (NB - early) // len(CHUNKS)))
            sort_turns(1, between)

            act.wait_ge(s_edge0, 2)
            for g in range(GPI):
                feed(0, 0, g)

            def attention(i, first):
                for g in range(GPI):
                    p = g % 2
                    G0 = i * GPI + g
                    act.wait_ge(s_got[0][g], i * 64 + 64)
                    feed(0, i + 1, g)
                    act.wait_ge(s_score, G0 + 1)
                    if not (first and g < 2):
                        act.wait_ge(s_part[0], G0 - 1)
                    nc.scalar.activation(msg[:, p, :, D:MSG],
                                         score[:, p, :].rearrange("p (t h) -> p t h", h=HEADS),
                                         ACT.Exp).then_inc(s_exp, 1)
                    act.wait_ge(s_hotp, G0 + 3)
                    act.wait_ge(s_q, G0 + 1)
                    nc.scalar.copy(hotT[:, p, :], turned_hot[p]).then_inc(s_hotT, 1)
                    widen((g + 2) % 4, G0 + 2, first and g < 2)

            def widen(place, G0, first):
                act.wait_ge(s_hot[0], G0 + 1)
                if not first:
                    act.wait_ge(s_part[0], G0 - (GPI - 1))
                nc.scalar.copy(hot[:, place, :, :], hot_b[:, place, :, :]).then_inc(s_wide, 1)

            for u in range(2):
                act.wait_ge(s_tab[0][u], 16 * (NS // PER))
            for n in range(2):
                act.wait_ge(s_hotp, n + 1)
                nc.scalar.copy(hotT[:, n, :], turned_hot[n]).then_inc(s_hotT, 1)
                widen(n, n, True)
            attention(0, True)
            with act.Fori(1, ITERS) as i:
                attention(i, False)

            act.wait_ge(s_degr, 1)
            nc.scalar.activation(root[:], deg[:], ACT.Sqrt).then_inc(s_degroot, 1)
            act.wait_ge(s_rows, 16 * GROUPS)
            act.wait_ge(s_hot[0], NT // GRP + 3)
            for g in range(GROUPS + 1):
                if g >= 1:
                    act.wait_ge(s_rowT, g)
                if g < GROUPS:
                    T = P if g < GROUPS - 1 else TAIL
                    nc.scalar.copy(rows_f[0:T, :], rows[0:T, g, :]).then_inc(s_rowf, 1)
                if g >= 1:
                    T = P if g - 1 < GROUPS - 1 else TAIL
                    c = slice((g - 1) * P, (g - 1) * P + T)
                    nc.scalar.copy(key_l[:, c], psA[(g - 1) % 2][:, 0:T])
                    nc.scalar.copy(partner[:, c], psA[(g - 1) % 2][:, P:P + T]).then_inc(s_rowk, 1)
            root_of(1, 0)
            act.wait_ge(s_dinv, 1)
            act.wait_ge(s_list1, 16)
            project_chunk = projection(1)
            project_chunk(0, first=True)
            with act.Fori(1, len(CHUNKS) - 1) as i:
                project_chunk(i)
            project_chunk(len(CHUNKS) - 1, last=True)

            act.wait_ge(s_rowk, GROUPS)
            for g in range(GPI):
                feed(1, 0, g)

            def feeds(i, skip, first=False):
                for g in range(GPI):
                    act.wait_ge(s_got[1][g], i * 64 + 64)
                    feed(1, i + 1, g)
                    if skip and g == 0:
                        if not first:
                            act.wait_ge(s_sT, i)
                        nc.scalar.copy(stage[:, 0, 0, :], H[:, bass.ds(i, 1), :].rearrange("p a d -> p (a d)")
                                       ).then_inc(s_sstage, 1)
                    if skip and g == 2:
                        act.wait_ge(s_sT, i + 1)
                        if not first:
                            act.wait_ge(s_smm, i)
                        nc.scalar.copy(hT[:, 0, :], psA[0][0:D, 0:P]).then_inc(s_shT, 1)

            feeds(0, True, True)
            with act.Fori(1, NS) as i:
                feeds(i, True)
            with act.Fori(NS, ITERS) as i:
                feeds(i, False)

            for n, (b0, b1) in enumerate(CHUNKS):
                act.wait_ge(s_y, n + 1)
                nc.scalar.activation(H[:, b0:b1, :], G[:, b0:b1, :], ACT.Exp).then_inc(s_ye, 1)
                act.wait_ge(s_ye, n + 1)
                nc.scalar.activation(G[:, b0:b1, :], H[:, b0:b1, :], ACT.Square, bias=ones[:, 0:1]).then_inc(s_esq, 1)
                act.wait_ge(s_esq, n + 1)
                nc.scalar.activation(G[:, b0:b1, :], G[:, b0:b1, :], ACT.Identity, bias=ones[:, 0:1]).then_inc(s_den, 1)

        @block.tensor
        def _(pe):
            pe.wait_ge(s_const, 1)

            def sort_turns(k, between):
                for s in range(ACROSS):
                    for h in range(2):
                        pe.wait_ge(s_plain[k][h], s + 1)
                        for n in range(TURNS):
                            c = h * HALF + n * P
                            mm = nc.tensor.transpose(psA[h][:, n:P * TURNS:TURNS], plain[:, c:c + P], ident[:])
                        mm.then_inc(s_turn[k][h], 1)
                    for h in range(2):
                        pe.wait_ge(s_cross[k][h], s + 1)
                        for n in range(TURNS):
                            mm = nc.tensor.transpose(psB[h][:, n * P:(n + 1) * P], turned[0][:, h, n:P * TURNS:TURNS],
                                                     ident[:])
                        mm.then_inc(s_back[k][h], 1)
                    between(s)

            pe.wait_ge(s_flagd, 1)
            nc.tensor.matmul(psD[:, 0:1], ones[:], flag[:, 0:1], start=True, stop=True).then_inc(s_flagp, 1)
            pe.wait_ge(s_flag, 1)
            unsorted = pe.value_load(flag_i[0:1, 0:1], min_val=0, max_val=1)
            with pe.If(unsorted > 0):
                sort_turns(0, lambda s: None)
            with pe.Else():
                pe.wait_ge(s_flag, 1)

            def projection(k, weights, width):
                def turn(b, j, i, first):
                    if j % UNIT == 0:
                        pe.wait_ge(s_pstage[k], i * 2 + (j // UNIT + 1))
                    if not (first and j < 2):
                        pe.wait_ge(s_phT[k], b - 1)
                    nc.tensor.transpose(psA[j % 2][0:D, 0:P], stage[:, j // UNIT, j % UNIT, :], ident[:]).then_inc(s_pT[k], 1)

                def chunk(i, first):
                    turn(i * PER, 0, i, first)
                    for j in range(PER):
                        b = i * PER + j
                        if j + 1 < PER:
                            turn(b + 1, j + 1, i, first)
                        pe.wait_ge(s_phT[k], b + 1)
                        if not (first and j < 2):
                            pe.wait_ge(s_pkv[k], b - 1)
                        nc.tensor.matmul(psB[j % 2][:, 0:width], hT[:, j % 2, :], weights[:, 0:width],
                                         start=True, stop=True).then_inc(s_pmm[k], 1)

                return chunk

            pe.wait_ge(s_w, 16 * 7)
            project_chunk = projection(0, qkv_w, 3 * D)

            def between(s):
                if s < len(CHUNKS):
                    project_chunk(s, s == 0)
                if s == len(CHUNKS) - 1:
                    pe.wait_ge(s_a, 2 * NB)
                    nc.tensor.matmul(psE[:, 0:2 * NB], ones[:], over[:, :, :].rearrange("p k b -> p (k b)"),
                                     start=True, stop=True).then_inc(s_above, 1)
                if s == len(CHUNKS):
                    pe.wait_ge(s_cols, 2)
                    nc.tensor.transpose(psE[:, P:2 * P], tile_end[:, :, :].rearrange("p k b -> p (k b)"), ident[:])
                    nc.tensor.transpose(psE[:, 2 * P:3 * P], shift[:, :, :].rearrange("p k b -> p (k b)"),
                                        ident[:]).then_inc(s_colT, 1)
                if s == len(CHUNKS) + 1:
                    pe.wait_ge(s_begun, 1)
                    for k in range(2):
                        side = slice(k * SIDE, k * SIDE + NB)
                        for m in range(2):
                            nc.tensor.matmul(bucket_ps[k][m][:, 0:HT], ones[side, :], begun[side, m * HT:(m + 1) * HT],
                                             start=True, stop=True)
                        for g in range(GROUPS):
                            mm = nc.tensor.matmul(bucket_ps[k][0][:, HT + g:HT + g + 1],
                                                  begun[side, g * P:(g + 1) * P], cols[side, 1:2], start=True, stop=True)
                    mm.then_inc(s_tile, 1)
            assert len(CHUNKS) + 1 < ACROSS
            sort_turns(1, between)

            for h in range(2):
                n_rows = FIRST_ROWS if h == 0 else GROUPS - FIRST_ROWS
                pe.wait_ge(s_rows0[h], 16 * n_rows)
                for n in range(n_rows):
                    g = h * FIRST_ROWS + n
                    T = P if g < GROUPS - 1 else TAIL
                    mm = nc.tensor.transpose(psA[h][:, n * P:n * P + T], rows[0:T, g, 0:P].bitcast(F32), ident[0:T, 0:T])
                mm.then_inc(s_turned0, 1)

            def turn_hot(g, G0):
                pe.wait_ge(s_hot[0], G0 + 1)
                for j in range(GRP):
                    mm = nc.tensor.transpose(turned_hot[g % 2][:, j * P:(j + 1) * P], hot_b[:, g, j, :], ident_b[:])
                mm.then_inc(s_hotp, 1)

            regs = [pe.alloc_register(f"tile_bucket{j}") for j in range(TPI)]

            def load_buckets(at, n):
                pe.load(regs[0:n], tile_b0[0:1, bass.ds(at, n)])
                return [pe.snap(r, min_val=0, max_val=NB) for r in regs[0:n]]

            def queries(p, buckets, G0):
                pe.wait_ge(s_hotT, G0 + 1)
                for j in range(GRP):
                    b = buckets[j]
                    mm = nc.tensor.matmul(psB[p][:, j * D:(j + 1) * D], hotT[:, p, j * P:(j + 1) * P],
                                          Q[:, bass.ds(b, 1), :].rearrange("p a d -> p (a d)"), start=True, stop=True)
                mm.then_inc(s_q, 1)

            def attention(i, first):
                buckets = load_buckets(i * TPI + (LEAD + GRP), TPI)
                for g in range(GPI):
                    p = g % 2
                    G0 = i * GPI + g
                    if not (first and g == 0):
                        pe.wait_ge(s_prod, G0)
                    queries(1 - p, buckets[g * GRP:(g + 1) * GRP], G0 + 1)
                    pe.wait_ge(s_hotT, G0 + 1)
                    turn_hot((g + 2) % 4, G0 + 2)
                    pe.wait_ge(s_hots, G0 + 1)
                    for j in range(GRP):
                        mm = nc.tensor.matmul(psD[:, 0:NS], low_hot[:, j, :], bkt_hot[:, j, :],
                                              start=False, stop=False, skip_group_check=True)
                    mm.then_inc(s_degmm, 1)
                    pe.wait_ge(s_msg, G0 + 1)
                    pe.wait_ge(s_wide, G0 + 1)
                    if not (first and g < 2):
                        pe.wait_ge(s_add[0], G0 * GRP + (1 - GRP))
                    for j in range(GRP):
                        mm = nc.tensor.matmul(psC[p][:, j * MSG:(j + 1) * MSG], hot[:, g, j, :], msg[:, p, j, :],
                                              start=True, stop=True)
                    mm.then_inc(s_part[0], 1)

            pe.wait_ge(s_tiled, 1)
            nc.tensor.matmul(psD[:, 0:NS], zero_b[:], zero_b[:, 0:NS], start=True, stop=False, skip_group_check=True)
            turn_hot(0, 0)
            turn_hot(1, 1)
            queries(0, load_buckets(LEAD, GRP), 0)
            attention(0, True)
            with pe.Fori(1, ITERS) as i:
                attention(i, False)

            for g in range(GROUPS):
                T = P if g < GROUPS - 1 else TAIL
                pe.wait_ge(s_rowf, g + 1)
                if g >= 2:
                    pe.wait_ge(s_rowk, g - 1)
                nc.tensor.transpose(psA[g % 2][:, 0:T], rows_f[0:T, 0:2 * P:2], ident[0:T, 0:T])
                nc.tensor.transpose(psA[g % 2][:, P:P + T], rows_f[0:T, 1:2 * P:2],
                                    ident[0:T, 0:T]).then_inc(s_rowT, 1)

            project_chunk = projection(1, gl_w, D)
            project_chunk(0, True)
            with pe.Fori(1, len(CHUNKS)) as i:
                project_chunk(i, False)
            def convolve(i, first, skip):
                for g in range(GPI):
                    p = g % 2
                    G0 = i * GPI + g
                    pe.wait_ge(s_hot[1], G0 + 1)
                    pe.wait_ge(s_got[1][g], i * 64 + 64)
                    if not (first and g < 2):
                        pe.wait_ge(s_add[1], G0 * GRP + (1 - GRP))
                    for j in range(GRP):
                        mm = nc.tensor.matmul(psC[p][:, j * D:(j + 1) * D], hot[:, g, j, :],
                                              got[:, g * GRP + j, 0:D], start=True, stop=True)
                    mm.then_inc(s_part[1], 1)
                    if skip and g == 1:
                        pe.wait_ge(s_sstage, i + 1)
                        if not first:
                            pe.wait_ge(s_shT, i)
                        nc.tensor.transpose(psA[0][0:D, 0:P], stage[:, 0, 0, :], ident[:]).then_inc(s_sT, 1)
                    if skip and g == 3:
                        pe.wait_ge(s_shT, i + 1)
                        if not first:
                            pe.wait_ge(s_skip, i)
                        nc.tensor.matmul(psB[0][:, 0:D], hT[:, 0, :], gl_w[:, D:2 * D], start=True, stop=True
                                         ).then_inc(s_smm, 1)

            convolve(0, True, True)
            with pe.Fori(1, NS) as i:
                convolve(i, False, True)
            with pe.Fori(NS, ITERS) as i:
                convolve(i, False, False)

        @block.vector
        def _(dve):
            v = Chain(dve, s_v)

            for t in (src_i[:], dst_i[:], nxt_i):
                nc.vector.memset(t, PAD_KEY)
            nc.vector.memset(X[:, FULL:NS, :], 0.0)
            nc.vector.memset(ones[:], 1.0)
            nc.vector.memset(zero_b[:], 0.0).then_inc(s_pads, 1)
            nc.vector.memset(bkt_b[:, NCOL:NT], 63.0)
            v.link(nc.vector.memset(low_b[:, NCOL:NT], 255.0))
            dve.wait_ge(s_iota, 5)
            nc.vector.tensor_scalar(ident[:], diff[:], 0.0, None, ALU.is_equal)
            nc.vector.tensor_scalar(ident_b[:], diff[:], 0.0, None, ALU.is_equal)
            nc.vector.tensor_copy(iota_b[:], iota_n[:])
            for lev in range(ACROSS + 1):
                ins = nc.vector.tensor_scalar(sign_i[:, lev:lev + 1], lane_i[:, 0:1], lev, 1, ALU.arith_shift_right,
                                              ALU.bitwise_and)
            v.link(ins)
            v.link(nc.vector.tensor_scalar(signs[:], sign_i[:], 2.0, -1.0, ALU.mult, ALU.add))
            v.link(nc.vector.memset(signs[:, ACROSS:ACROSS + 1], 1.0))
            nc.vector.tensor_scalar(bounds[:], iota_n[:, 0:NB], -float(P), 0.5 - P, ALU.mult, ALU.add).then_inc(s_const, 1)
            dve.wait_ge(s_const, 1)

            def pack(key, partner_of):
                ki = keys[0].bitcast(I32)
                nc.vector.memset(ki[:, NCOL:LANE], NEVER)
                v.link(nc.vector.tensor_scalar(ki[:, 0:NCOL], key[:], NODE_BITS, 1 << NORMAL_BIT,
                                               ALU.logical_shift_left, ALU.bitwise_or))
                v.link(nc.vector.tensor_tensor(ki[:, 0:NCOL], ki[:, 0:NCOL], partner_of[:], ALU.bitwise_or))

            def sort(k, between):
                c = Chain(dve, s_chain[k])
                at = 0

                def order(src_ap, dst_ap, k_, outer, descending, after, upper=None, done=None):
                    if after:
                        dve.wait_ge(s_chain[k], after)
                    if descending is None:
                        a = [t.rearrange("p (g two k) -> p g two k", two=2, k=k_)
                             for t in (src_ap, dst_ap, src_ap if upper is None else upper)]
                        lo = [a[0][:, :, 0, :], a[1][:, :, 0, :]]
                        hi = [a[2][:, :, 1, :], a[1][:, :, 1, :]]
                    else:
                        q = 0 if descending else 1
                        a = [t.rearrange("p (b side g two k) -> p b side g two k", side=2, two=2, k=k_,
                                         g=outer // (2 * k_))
                             for t in (src_ap, dst_ap, src_ap if upper is None else upper)]
                        lo = [a[0][:, :, q, :, 0, :], a[1][:, :, q, :, 0, :]]
                        hi = [a[2][:, :, q, :, 1, :], a[1][:, :, q, :, 1, :]]
                    least, most = (hi, lo) if descending else (lo, hi)
                    c(nc.vector.tensor_tensor(least[1], lo[0], hi[0], ALU.min))
                    larger = nc.vector.tensor_tensor(most[1], lo[0], hi[0], ALU.max)
                    if done:
                        larger.then_inc(done, 1)
                    else:
                        c(larger)
                    return c.n

                ready = [0, 0]
                for lev in range(1, IN_LANE):
                    start = max(ready)
                    ready = [start, start]
                    for e in reversed(range(lev)):
                        for d in range(2):
                            ready[d] = order(keys[at], keys[1 - at], 1 << e, 1 << lev, 1 - d, ready[d])
                        at = 1 - at
                between(-1)
                dve.wait_ge(s_chain[k], max(ready))
                c(nc.vector.tensor_scalar(keys[1 - at], keys[at], signs[:, 0:1], None, ALU.mult))
                at = 1 - at
                ready = [c.n, c.n]
                for s in range(ACROSS + 1):
                    if s > 0:
                        for h in range(2):
                            dve.wait_ge(s_turn[k][h], s)
                            source, upper = psA[h][:, :], turned[s % 2][:, h, :]
                            view = "p (g two k) -> p g two k"
                            c(nc.vector.tensor_copy(upper.rearrange(view, two=2, k=TURNS << (s - 1))[:, :, 1, :],
                                                    source.rearrange(view, two=2, k=TURNS << (s - 1))[:, :, 1, :]))
                            after = c.n
                            for e in reversed(range(s)):
                                to = turned[e % 2][:, h, :]
                                done = None if e else s_cross[k][h]
                                if s < ACROSS:
                                    order(source, to, TURNS << e, TURNS << s, True, after, upper)
                                    after = order(source, to, TURNS << e, TURNS << s, False, 0, upper, done)
                                else:
                                    after = order(source, to, TURNS << e, 0, None, after, upper, done)
                                source, upper = to, None
                        for h in range(2):
                            dve.wait_ge(s_signed[k][h], s)
                        at = 0
                        ready = [c.n, c.n]
                    ready[0] = ready[1] = order(keys[at], keys[1 - at], HALF, 0, None, max(ready))
                    at = 1 - at
                    start_at = at
                    steps = [(e, h) for e in reversed(range(ALONE, IN_LANE - 1)) for h in range(2)]
                    steps += [(e, h) for h in range(2) for e in reversed(range(ALONE))]
                    for e, h in steps:
                        src_b = (start_at + (IN_LANE - 2 - e)) % 2
                        cut = slice(h * HALF, (h + 1) * HALF)
                        assert e > 0 or src_b == 1
                        ready[h] = order(keys[src_b][:, cut], keys[1 - src_b][:, cut], 1 << e, 0, None, ready[h],
                                         done=None if e else s_lane[k][h])
                    at = 0
                    between(s)

            def shared_rows():
                dve.wait_ge(s_above, 1)
                for t in (tile_end, shift):
                    nc.vector.memset(t[:, :, :], 0.0)
                v.link(nc.vector.memset(above[:, :, :], 0.0))
                v.link(nc.vector.memset(above[:, :, 0:1], float(P * NCOL)))
                v.link(nc.vector.tensor_scalar(above[:, :, 1:NS], psE[:, 0:2 * NB].rearrange("p (k b) -> p k b", k=2),
                                               0.5, 0.5 * P * NCOL, ALU.mult, ALU.add))
                v.link(nc.vector.tensor_tensor(n_all[:, :, :], above[:, :, 0:NS], above[:, :, 1:NS + 1], ALU.subtract))
                v.link(nc.vector.tensor_scalar(above[:, :, :], above[:, :, :], -1.0, float(P * NCOL), ALU.mult, ALU.add))
                for out_t, add in ((first_row, 0.0), (next_row, float(P - 1))):
                    v.link(nc.vector.tensor_scalar(start_i[:, :, :], above[:, :, :], add, None, ALU.add))
                    v.link(nc.vector.tensor_scalar(start_i[:, :, :], start_i[:, :, :], LOW_BITS, None, ALU.arith_shift_right))
                    v.link(nc.vector.tensor_copy(out_t[:, :, :], start_i[:, :, :]))
                v.link(nc.vector.tensor_tensor(n_tile[:, :, :], next_row[:, :, 1:NS + 1], first_row[:, :, 0:NS], ALU.subtract))
                v.link(nc.vector.scalar_tensor_tensor(out=n_tile[:, :, :], in0=n_all[:, :, :], scalar=0.0,
                                                      in1=n_tile[:, :, :], op0=ALU.is_gt, op1=ALU.mult))
                v.link(nc.vector.tensor_tensor(shift[:, :, 0:NS], first_row[:, :, 1:NS + 1], first_row[:, :, 0:NS], ALU.subtract))
                v.link(nc.vector.tensor_tensor(shift[:, :, 0:NS], shift[:, :, 0:NS], n_tile[:, :, :], ALU.subtract))
                for k in range(2):
                    nc.vector.tensor_tensor_scan(tile_end[:, k, 0:NS], ones[:, 0:NS], n_tile[:, k, :], 0.0,
                                                 ALU.mult, ALU.add).then_inc(s_cols, 1)

            def buckets_begun():
                dve.wait_ge(s_colT, 1)
                v.link(nc.vector.tensor_copy(cols[:, 0:1], psE[:, P:P + 1]))
                v.link(nc.vector.tensor_copy(cols[:, 1:2], psE[:, 2 * P:2 * P + 1]))
                nc.vector.tensor_scalar(begun, iota_t, cols[:, 0:1], None, ALU.is_ge).then_inc(s_begun, 1)

            def mean_off(b0, b1):
                cut = slice(b0, b1)
                v.link(nc.vector.tensor_reduce(mean[:, cut], X[:, cut, :], AX.X, ALU.add))
                v.link(nc.vector.tensor_scalar(mean[:, cut], mean[:, cut], 1.0 / D, None, ALU.mult))
                return nc.vector.tensor_tensor(H[:, cut, :], X[:, cut, :], wide(mean, b0, b1), ALU.subtract)

            def variance(k, b0, b1):
                cut = slice(b0, b1)
                v.link(nc.vector.tensor_reduce(var[:, cut], T1[:, cut, :], AX.X, ALU.add))
                nc.vector.tensor_scalar(var[:, cut], var[:, cut], 1.0 / D, EPS, ALU.mult, ALU.add).then_inc(s_var[k], 1)

            def inverse_root(k, b0, b1, n=0):
                dve.wait_ge(s_root[k], n + 1)
                return nc.vector.reciprocal(rstd[:, b0:b1], rstd[:, b0:b1])

            dve.wait_ge(s_edges, 16 * 6)
            di = gotf[:, 0:LANE].bitcast(I32)
            dj = gotf[:, LANE:2 * LANE].bitcast(I32)
            v.link(nc.vector.tensor_scalar(di[:, 0:NCOL], dst_i[:], LOW_BITS, None, ALU.arith_shift_right))
            v.link(nc.vector.tensor_scalar(nxt_i, nxt_i, LOW_BITS, None, ALU.arith_shift_right))
            v.link(nc.vector.tensor_tensor(dj[:, 0:NCOL], di[:, 0:NCOL], nxt_i, ALU.is_gt))
            nc.vector.tensor_reduce(flag[:, 0:1], dj[:, 0:NCOL], AX.X, ALU.add).then_inc(s_flagd, 1)
            nc.vector.tensor_copy(pair1[:, :, 0], dst_i[:])
            nc.vector.tensor_copy(pair1[:, :, 1], src_i[:]).then_inc(s_pair, 1)
            dve.wait_ge(s_flagp, 1)
            nc.vector.tensor_scalar(flag_i[:], psD[0:1, 0:1], 1.0, None, ALU.min).then_inc(s_flag, 1)
            dve.wait_ge(s_flag, 1)
            unsorted = dve.value_load(flag_i[0:1, 0:1], min_val=0, max_val=1)
            v0 = v
            with dve.If(unsorted > 0):
                v = Chain(dve, s_vf)
                pack(dst_i, src_i)
                sort(0, lambda s: None)
                for h in range(2):
                    dve.wait_ge(s_lane[0][h], ACROSS + 1)
                ki = keys[0].bitcast(I32)
                nc.vector.tensor_scalar(back_pair[:, :, 1], ki, ANY_NODE, None, ALU.bitwise_and)
                nc.vector.tensor_scalar(back_pair[:, :, 0], ki, NODE_BITS, ANY_NODE,
                                        ALU.logical_shift_right, ALU.bitwise_and).then_inc(s_pair, 1)
                dve.wait_ge(s_pair, 2)
            with dve.Else():
                dve.wait_ge(s_flag, 1)
            v = v0

            pack(src_i, dst_i)

            def between(s):
                if s < 0:
                    inverse_root(0, 0, NS).then_inc(s_stat, 1)
                if s == len(CHUNKS):
                    shared_rows()
                if s == len(CHUNKS) + 1:
                    buckets_begun()
            sort(1, between)

            dve.wait_ge(s_tile, 1)
            for k in range(2):
                nc.vector.tensor_tensor(tile_row[:, k, :], bucket_ps[k][0][:, HT:HT + GROUPS],
                                        tile_iota[:], ALU.add).then_inc(s_chain_rows, 1)
            dve.wait_ge(s_chain_rows, 2)
            nc.vector.tensor_scalar(tile_row_i[:, :, :], tile_row[:, :, :], float(NCOL - 1), None, ALU.min
                                    ).then_inc(s_rowidx, 1)
            nc.vector.memset(tile_b0[:, 0:LEAD], NB)
            nc.vector.memset(tile_b1[:, 0:LEAD], NB)
            for m in range(2):
                half = slice(m * HT, (m + 1) * HT)
                nc.vector.tensor_scalar(key_l[:, half], psC[m][:, 0:HT], -float(P), None, ALU.mult)
                nc.vector.tensor_scalar(base1[:, half], bucket_ps[1][m][:, 0:HT], float(P), None, ALU.mult)
                nc.vector.tensor_copy(tile_b0[:, LEAD + m * HT:LEAD + (m + 1) * HT], psC[m][0:1, 0:HT])
                ins = nc.vector.tensor_copy(tile_b1[:, LEAD + m * HT:LEAD + (m + 1) * HT], bucket_ps[1][m][0:1, 0:HT])
            ins.then_inc(s_tiled, 1)
            dve.wait_ge(s_tiled, 1)
            v.link(nc.vector.tensor_scalar(di[:, 0:NCOL], dst_i[:], LOW_BITS, None, ALU.arith_shift_right))
            v.link(nc.vector.tensor_copy(bkt_b[:, 0:NCOL], di[:, 0:NCOL]))
            v.link(nc.vector.tensor_scalar(di[:, 0:NCOL], dst_i[:], P - 1, None, ALU.bitwise_and))
            v.link(nc.vector.tensor_copy(low_b[:, 0:NCOL], di[:, 0:NCOL]))
            nc.vector.memset(partner[:, NT:NTP], 0)
            nc.vector.memset(key_l[:, NT:NTP], float(2 * P))
            nc.vector.memset(sums[:, :, :], 0.0).then_inc(s_add[0], 1)
            for h in range(2):
                at = slice(h * FIRST_ROWS * P, min((h + 1) * FIRST_ROWS * P, NT))
                turned_keys = psA[h][:, 0:at.stop - at.start].bitcast(I32)
                dve.wait_ge(s_turned0, h + 1)
                nc.vector.tensor_scalar(partner[:, at], turned_keys, ANY_NODE, None, ALU.bitwise_and)
                v.link(nc.vector.tensor_scalar(node_i[:, at], turned_keys, NODE_BITS, ANY_NODE,
                                               ALU.logical_shift_right, ALU.bitwise_and))
                nc.vector.tensor_tensor(key_l[:, at], key_l[:, at], node_i[:, at], ALU.add).then_inc(s_edge0, 1)
            dve.wait_ge(s_edge0, 2)

            def one_hots(k, g, i, off):
                for j in range(GRP):
                    ins = nc.vector.tensor_scalar((hot if k else hot_b)[:, g, j, :], (iota_n if k else iota_b)[:],
                                                  key_l[:, bass.ds(i * TPI + (off * GRP + j), 1)], None, ALU.is_equal)
                ins.then_inc(s_hot[k], 1)

            regs = [dve.alloc_register(f"tile_bucket{j}") for j in range(TPI)]

            def load_buckets(tile_b, at, n):
                dve.load(regs[0:n], tile_b[0:1, bass.ds(at, n)])
                return [dve.snap(r, min_val=0, max_val=NB) for r in regs[0:n]]

            def add_part(k, bucket, width, p, j, G0):
                at = sums[:, bass.ds(bucket, 1), 0:width].rearrange("p a d -> p (a d)")
                dve.wait_ge(s_add[k], G0 * GRP + (j + 1))
                nc.vector.tensor_tensor(at, at, psC[p][:, j * width:(j + 1) * width], ALU.add).then_inc(s_add[k], 1)

            def add_parts(k, buckets, width, p, G0):
                dve.wait_ge(s_part[k], G0 + 1)
                for j in range(GRP):
                    add_part(k, buckets[j], width, p, j, G0)

            def attention(i, first):
                buckets = load_buckets(tile_b0, i * TPI, TPI)
                for g in range(GPI):
                    p = g % 2
                    G0 = i * GPI + g
                    ahead = (g + 3) % 4

                    def one_hot(j):
                        return nc.vector.tensor_scalar(hot_b[:, ahead, j, :], iota_b[:],
                                                       key_l[:, bass.ds(i * TPI + ((g + 3) * GRP + j), 1)], None, ALU.is_equal)

                    def low_one_hot(j):
                        return nc.vector.tensor_scalar(low_hot[:, j, :], iota_b[:],
                                                       low_b[:, bass.ds(i * TPI + (g * GRP + j), 1)], None, ALU.is_equal)

                    def add(j):
                        if not (first and g < 2):
                            add_part(0, buckets[g * GRP + j], MSG, p, j, G0 - 2)

                    dve.wait_ge(s_q, G0 + 1)
                    dve.wait_ge(s_got[0][g], i * 64 + 64)
                    rows4 = got[:, g * GRP:(g + 1) * GRP, :]
                    nc.vector.tensor_tensor(prod, psB[p][:, 0:GRP * D].rearrange("p (t d) -> p t d", d=D),
                                            rows4[:, :, 0:D], ALU.mult).then_inc(s_prod, 1)
                    if not (first and g < 2):
                        dve.wait_ge(s_part[0], G0 - 1)
                    add(0)
                    if not (first and g == 0):
                        dve.wait_ge(s_degmm, G0)
                    columns = bkt_b[:, bass.ds(i * TPI + g * GRP, GRP)].rearrange("p (c a) -> p c a", a=1)
                    nc.vector.tensor_tensor(
                        bkt_hot[:], iota_b[:, 0:NS].rearrange("p (a n) -> p a n", a=1).to_broadcast([P, GRP, NS]),
                        columns.to_broadcast([P, GRP, NS]), ALU.is_equal)
                    add(1)
                    dve.wait_ge(s_prod, G0 + 1)
                    if not (first and g < 2):
                        dve.wait_ge(s_exp, G0 - 1)
                    nc.vector.tensor_reduce(score[:, p, :], prod.rearrange("p t (h d) -> p (t h) d", d=DH),
                                            AX.X, ALU.add).then_inc(s_red, 1)
                    add(2)
                    low_one_hot(0)
                    dve.wait_ge(s_red, G0 + 1)
                    nc.vector.tensor_scalar(score[:, p, :], score[:, p, :], -CLIP, CLIP, ALU.max, ALU.min
                                            ).then_inc(s_score, 1)
                    low_one_hot(1)
                    add(3)
                    low_one_hot(2)
                    low_one_hot(3).then_inc(s_hots, 1)
                    if not (first and g == 0):
                        dve.wait_ge(s_hotp, G0)
                        dve.wait_ge(s_wide, G0)
                    for j in range(GRP):
                        ins = one_hot(j)
                    ins.then_inc(s_hot[0], 1)
                    dve.wait_ge(s_exp, G0 + 1)
                    nc.vector.tensor_tensor(
                        msg[:, p, :, 0:D].rearrange("p t (h d) -> p t h d", h=HEADS),
                        rows4[:, :, D:2 * D].rearrange("p t (h d) -> p t h d", h=HEADS),
                        msg[:, p, :, D:MSG].rearrange("p t (h a) -> p t h a", a=1).to_broadcast([P, GRP, HEADS, DH]),
                        ALU.mult).then_inc(s_msg, 1)

            one_hots(0, 0, 0, 0)
            one_hots(0, 1, 0, 1)
            one_hots(0, 2, 0, 2)
            attention(0, True)
            with dve.Fori(1, ITERS) as i:
                attention(i, False)
            last = NT // GRP - 1
            buckets = load_buckets(tile_b0, NT, 2 * GRP)
            add_parts(0, buckets[0:GRP], MSG, (last - 1) % 2, last - 1)
            add_parts(0, buckets[GRP:2 * GRP], MSG, last % 2, last)

            dve.wait_ge(s_degmm, NT // GRP)
            nc.vector.tensor_scalar(deg[:], psD[:, 0:NS], 1.0, None, ALU.add).then_inc(s_degr, 1)
            dve.wait_ge(s_add[0], NT + 1)
            dve.wait_ge(s_xh, 1)
            weights = sums[:, :, D:MSG]
            v.link(nc.vector.tensor_scalar(weights, weights, 1e-8, None, ALU.add))
            v.link(nc.vector.reciprocal(weights, weights))
            dve.wait_ge(s_degroot, 1)
            nc.vector.reciprocal(dinv[:], root[:]).then_inc(s_dinv, 1)
            for n in range(len(CHUNKS) + 1):
                if n < len(CHUNKS):
                    b0, b1 = CHUNKS[n]
                    v.link(nc.vector.tensor_tensor(
                        T1[:, b0:b1, :].rearrange("p b (h d) -> p b h d", h=HEADS),
                        sums[:, b0:b1, 0:D].rearrange("p b (h d) -> p b h d", h=HEADS),
                        weights[:, b0:b1, :].rearrange("p b (h a) -> p b h a", a=1).to_broadcast([P, PER, HEADS, DH]),
                        ALU.mult))
                    v.link(nc.vector.tensor_tensor(X[:, b0:b1, :], X[:, b0:b1, :], T1[:, b0:b1, :], ALU.add))
                    v.link(mean_off(b0, b1))
                    v.link(nc.vector.tensor_tensor(T1[:, b0:b1, :], H[:, b0:b1, :], H[:, b0:b1, :], ALU.mult))
                    variance(1, b0, b1)
                if n >= 1:
                    b0, b1 = CHUNKS[n - 1]
                    v.link(inverse_root(1, b0, b1, n - 1))
                    nc.vector.scalar_tensor_tensor(out=H[:, b0:b1, :], in0=H[:, b0:b1, :], scalar=0.0,
                                                   in1=wide(rstd, b0, b1), op0=ALU.max, op1=ALU.mult).then_inc(s_act[1], 1)
            nc.vector.memset(sums[:, :, :], 0.0).then_inc(s_add[1], 1)
            dve.wait_ge(s_rowk, GROUPS)
            v.link(nc.vector.tensor_tensor(key_l[:, 0:NT], key_l[:, 0:NT], base1[:, 0:NT], ALU.subtract))

            dve.wait_ge(s_w, 16 * 7)
            dve.wait_ge(s_pkv[1], NS)
            v.link(nc.vector.tensor_tensor(bias2[:, 0, :], bias2[:, 0, :], bias2[:, 1, :], ALU.add))

            def skip_branch(b, step):
                at = Q[:, bass.ds(b, 1), :].rearrange("p a d -> p (a d)")
                if step == 0:
                    dve.wait_ge(s_smm, b + 1)
                    nc.vector.scalar_tensor_tensor(
                        out=at, in0=G[:, bass.ds(b, 1), :].rearrange("p a d -> p (a d)"), scalar=dinv[:, bass.ds(b, 1)],
                        in1=psB[0][:, 0:D], op0=ALU.mult, op1=ALU.add).then_inc(s_skip, 1)
                else:
                    dve.wait_ge(s_skip, b + 1)
                    nc.vector.tensor_tensor(at, at, bias2[:, 0, :], ALU.add).then_inc(s_addend, 1)

            def convolve(i, first, addend):
                buckets = load_buckets(tile_b1, i * TPI + (LEAD - GRP), TPI)
                for g in range(GPI):
                    p = g % 2
                    G0 = i * GPI + g
                    if not first:
                        dve.wait_ge(s_part[1], G0 - (GPI - 1))
                    one_hots(1, g, i, g)
                    if addend and g < 2 and not (first and g < 2):
                        skip_branch(i - 1, g)
                    if not (first and g == 0):
                        add_parts(1, buckets[g * GRP:(g + 1) * GRP], D, 1 - p, G0 - 1)

            convolve(0, True, True)
            with dve.Fori(1, NS) as i:
                convolve(i, False, True)
            skip_branch(NS - 1, 0)
            skip_branch(NS - 1, 1)
            with dve.Fori(NS, ITERS) as i:
                convolve(i, False, False)
            add_parts(1, load_buckets(tile_b1, NT + (LEAD - GRP), GRP), D, last % 2, last)

            dve.wait_ge(s_add[1], NT + 1)
            dve.wait_ge(s_addend, NS)
            for n in range(len(CHUNKS) + 1):
                if n < len(CHUNKS):
                    b0, b1 = CHUNKS[n]
                    y = T1[:, b0:b1, :]
                    v.link(nc.vector.tensor_tensor(y, sums[:, b0:b1, 0:D], wide(dinv, b0, b1), ALU.mult))
                    v.link(nc.vector.tensor_tensor(y, y, Q[:, b0:b1, :], ALU.add))
                    nc.vector.tensor_scalar(G[:, b0:b1, :], y, 20.0, None, ALU.min).then_inc(s_y, 1)
                if n >= 1:
                    b0, b1 = CHUNKS[n - 1]
                    e, r = H[:, b0:b1, :], G[:, b0:b1, :]
                    dve.wait_ge(s_den, n)
                    nc.vector.scalar_tensor_tensor(out=e, in0=e, scalar=2.0, in1=e, op0=ALU.add, op1=ALU.mult)
                    nc.vector.reciprocal(r, r).then_inc(s_mish, 1)


_INS = ["x", "src", "dst", "L0_gnn_qW", "L0_gnn_kW", "L0_gnn_vW", "L1_gnn_W_gcn", "L1_gnn_b_gcn",
        "L1_gnn_W_lin", "L1_gnn_b_lin"]


def kernel(**inputs):
    import numpy as _np
    import concourse.bacc as _bacc
    from concourse import mybir as _mybir
    from concourse.bass_utils import run_bass_kernel_spmd as _run

    nc = _bacc.Bacc("TRN2", target_bir_lowering=False, num_devices=1)
    arrays, args = {}, []
    for name in _INS:
        a = _np.ascontiguousarray(inputs[name])
        arrays[f"in_{name}"] = a
        args.append(nc.dram_tensor(f"in_{name}", a.shape, _mybir.dt.from_np(a.dtype), kind="ExternalInput").ap())
    args.append(nc.dram_tensor("out_x", inputs["x"].shape, _mybir.dt.float32, kind="ExternalOutput").ap())
    gnn_kernel(nc, *args)
    r = _run(nc, [arrays], core_ids=[0])
    return r.results[0]["out_x"]
```
